# Optimizing a Trainium2 kernel written in Bass

```python
import numpy as np
import jax
import jax.numpy as jnp

def _softmax(x, axis=-1):
    return jax.nn.softmax(x, axis=axis)

def _gelu(x):
    return jax.nn.gelu(x, approximate=True)

def _silu(x):
    return jax.nn.silu(x)

def _sigmoid(x):
    return jax.nn.sigmoid(x)

def _layernorm(x, axis=-1, eps=1e-05):
    m = jnp.mean(x, axis=axis, keepdims=True)
    v = jnp.var(x, axis=axis, keepdims=True)
    return (x - m) / jnp.sqrt(v + eps)

def _scatter_add(tgt, idx, src, axis=0):
    return tgt.at[idx].add(src)

def _segment_sum(src, seg, n):
    return jax.ops.segment_sum(src, seg, n)
kernel_name = 'mk_cond_resid_d2_seqx_r4_60e2be'

def setup_inputs(seed: int=0):
    np.random.seed(seed)
    _w = jnp.asarray

    def _rec_inputs():
        import jax
        import jax.numpy as jnp
        _rk = jax.random.key(seed)
        x = 7.22e-05 + 1 * jax.random.normal(jax.random.fold_in(_rk, 1), (128, 64, 256), jnp.float32)
        _lenS = 64 - jax.random.randint(jax.random.fold_in(_rk, 7), (128,), 0, max(1, 64 // 4) + 1, jnp.int32)
        _lenS2 = 64 - jax.random.randint(jax.random.fold_in(_rk, 8), (128,), 0, max(1, 64 // 4) + 1, jnp.int32)
        condB_tauraws = -5.74692 + 0.777674 * jax.random.normal(jax.random.fold_in(_rk, 11), (128,), jnp.float32)
        cond_256 = -0.000235209 + 0.019331 * jax.random.normal(jax.random.fold_in(_rk, 12), (128, 64), jnp.float32)
        condB_bn2 = jnp.zeros((128,), jnp.float32)
        cond_1024 = -4.10585e-05 + 0.0199478 * jax.random.normal(jax.random.fold_in(_rk, 14), (128, 256), jnp.float32)
        itok_B_0_8 = jax.random.randint(jax.random.fold_in(_rk, 15), (128,), 0, 9, jnp.int32)
        return (x, condB_tauraws, cond_256, condB_bn2, cond_1024, itok_B_0_8)
    x, condB_tauraws, cond_256, condB_bn2, cond_1024, itok_B_0_8 = _rec_inputs()

    def _L0_cond_setup():
        import jax, jax.numpy as jnp
        import numpy as np
        import math
        B, T, E, D = (4, 512, 256, 4)

        def _tau_init(t):
            a = 0.1 ** (1.0 / max(t - 1, 1))
            tt = -math.log(max(a, 1e-10))
            return math.log(math.exp(tt) - 1 + 1e-10)

        def causal_ema(b, tau_raw):
            alpha = jnp.exp(-jax.nn.softplus(tau_raw)).astype(b.dtype)

            def step(h, bt):
                h = alpha * h + bt
                return (h, h)
            h0 = jnp.zeros((b.shape[0], b.shape[2]), b.dtype)
            _, hs = jax.lax.scan(step, h0, jnp.swapaxes(b, 0, 1))
            return jnp.swapaxes(hs, 0, 1)
        key = jax.random.key(seed)
        ks = jax.random.split(key, 10)
        s = 0.02
        return {'x': jax.random.normal(ks[0], (B, T, E), jnp.float32), 'tau_ctx': jnp.float32(_tau_init(max(T // 2, 4))), 'tau_raws': jnp.array([_tau_init(max(T // 2 ** i, 2)) for i in range(D)], jnp.float32), 'Wg': jax.random.normal(ks[1], (E, 2 * E), jnp.float32) * s, 'bg': jnp.full((E,), -0.5, jnp.float32), 'Wn1': jax.random.normal(ks[2], (E // 4, E), jnp.float32) * s, 'bn1': jnp.zeros((E // 4,), jnp.float32), 'Wn2': jax.random.normal(ks[3], (D, E // 4), jnp.float32) * s, 'bn2': jnp.zeros((D,), jnp.float32), 'blend': jax.random.normal(ks[4], (D, E), jnp.float32) * s, 'Wsoma': jax.random.normal(ks[5], (E, E), jnp.float32) * s, 'bsoma': jnp.zeros((E,), jnp.float32), 'Wtemp': jax.random.normal(ks[6], (E, E), jnp.float32) * s, 'btemp': jnp.zeros((E,), jnp.float32), 'Wout': jax.random.normal(ks[7], (E, E), jnp.float32) * s, 'gamma': jnp.ones((E,), jnp.float32), 'beta': jnp.zeros((E,), jnp.float32)}
    _L0_cond_all = _L0_cond_setup()
    _L0_cond_in = {k: v for k, v in _L0_cond_all.items() if k in ('tau_ctx', 'Wg', 'bg', 'Wn1', 'bn1', 'Wsoma', 'bsoma', 'Wtemp', 'btemp', 'Wout', 'gamma', 'beta')}
    del _L0_cond_all

    def _L1_cond_setup():
        import jax, jax.numpy as jnp
        import numpy as np
        LN_EPS = 1e-05
        key = jax.random.key(seed)
        ks = jax.random.split(key, 8)
        B, S, H, A, L = (32, 512, 256, 64, 10)
        return {'hidden_states': jax.random.normal(ks[0], (B, S, H), dtype=jnp.float32), 'language_ids': jax.random.randint(ks[1], (B,), 0, L, dtype=jnp.int64), 'W1': jax.random.normal(ks[2], (L, H, A), dtype=jnp.float32) * (1.0 / np.sqrt(H)), 'b1': jnp.zeros((L, A), dtype=jnp.float32), 'W2': jax.random.normal(ks[3], (L, A, H), dtype=jnp.float32) * (1.0 / np.sqrt(A)), 'b2': jnp.zeros((L, H), dtype=jnp.float32), 'gamma': jnp.ones((L, H), dtype=jnp.float32), 'beta': jnp.zeros((L, H), dtype=jnp.float32)}
    _L1_cond_all = _L1_cond_setup()
    _L1_cond_in = {k: v for k, v in _L1_cond_all.items() if k in ('W1', 'b1', 'W2', 'b2', 'gamma', 'beta')}
    del _L1_cond_all
    return {'x': x, 'condB_tauraws': condB_tauraws, 'cond_256': cond_256, 'condB_bn2': condB_bn2, 'cond_1024': cond_1024, 'itok_B_0_8': itok_B_0_8, 'L0_cond_tau_ctx': _L0_cond_in['tau_ctx'], 'L0_cond_Wg': _L0_cond_in['Wg'], 'L0_cond_bg': _L0_cond_in['bg'], 'L0_cond_Wn1': _L0_cond_in['Wn1'], 'L0_cond_bn1': _L0_cond_in['bn1'], 'L0_cond_Wsoma': _L0_cond_in['Wsoma'], 'L0_cond_bsoma': _L0_cond_in['bsoma'], 'L0_cond_Wtemp': _L0_cond_in['Wtemp'], 'L0_cond_btemp': _L0_cond_in['btemp'], 'L0_cond_Wout': _L0_cond_in['Wout'], 'L0_cond_gamma': _L0_cond_in['gamma'], 'L0_cond_beta': _L0_cond_in['beta'], 'L1_cond_W1': _L1_cond_in['W1'], 'L1_cond_b1': _L1_cond_in['b1'], 'L1_cond_W2': _L1_cond_in['W2'], 'L1_cond_b2': _L1_cond_in['b2'], 'L1_cond_gamma': _L1_cond_in['gamma'], 'L1_cond_beta': _L1_cond_in['beta']}

def reference(x, condB_tauraws, cond_256, condB_bn2, cond_1024, itok_B_0_8, L0_cond_tau_ctx, L0_cond_Wg, L0_cond_bg, L0_cond_Wn1, L0_cond_bn1, L0_cond_Wsoma, L0_cond_bsoma, L0_cond_Wtemp, L0_cond_btemp, L0_cond_Wout, L0_cond_gamma, L0_cond_beta, L1_cond_W1, L1_cond_b1, L1_cond_W2, L1_cond_b2, L1_cond_gamma, L1_cond_beta):
    import jax
    import jax.numpy as jnp

    def _L0_cond_ref(x, tau_ctx, tau_raws, Wg, bg, Wn1, bn1, Wn2, bn2, blend, Wsoma, bsoma, Wtemp, btemp, Wout, gamma, beta):
        import jax, jax.numpy as jnp
        import numpy as np
        import math
        B, T, E, D = (4, 512, 256, 4)

        def _tau_init(t):
            a = 0.1 ** (1.0 / max(t - 1, 1))
            tt = -math.log(max(a, 1e-10))
            return math.log(math.exp(tt) - 1 + 1e-10)

        def causal_ema(b, tau_raw):
            alpha = jnp.exp(-jax.nn.softplus(tau_raw)).astype(b.dtype)

            def step(h, bt):
                h = alpha * h + bt
                return (h, h)
            h0 = jnp.zeros((b.shape[0], b.shape[2]), b.dtype)
            _, hs = jax.lax.scan(step, h0, jnp.swapaxes(b, 0, 1))
            return jnp.swapaxes(hs, 0, 1)
        ctx = causal_ema(x, tau_ctx)
        gate_in = jnp.concatenate([x, ctx], axis=-1)
        wg = jax.nn.sigmoid(jnp.einsum('btc,ec->bte', gate_in, Wg) + bg)
        gated = x * wg
        h1 = jax.nn.gelu(jnp.einsum('btc,hc->bth', x, Wn1) + bn1, approximate=False)
        mod = 0.5 + jax.nn.sigmoid(jnp.einsum('bth,dh->btd', h1, Wn2) + bn2)
        traces = jax.vmap(lambda tau, m: causal_ema(gated * m[..., None], tau))(tau_raws, jnp.moveaxis(mod, -1, 0))
        blend_w = jax.nn.softmax(blend, axis=0)
        temporal = jnp.einsum('dbtc,dc->btc', traces, blend_w)
        gate = jax.nn.sigmoid(jnp.einsum('btc,ec->bte', temporal, Wtemp) + btemp)
        soma = jax.nn.gelu(jnp.einsum('btc,ec->bte', x, Wsoma) + bsoma, approximate=False)
        out = jnp.einsum('btc,ec->bte', soma * gate, Wout)
        mu = out.mean(-1, keepdims=True)
        var = out.var(-1, keepdims=True)
        return (out - mu) / jnp.sqrt(var + 1e-05) * gamma + beta

    def _L1_cond_ref(hidden_states, language_ids, W1, b1, W2, b2, gamma, beta):
        import jax, jax.numpy as jnp
        import numpy as np
        LN_EPS = 1e-05
        w1 = W1[language_ids]
        w2 = W2[language_ids]
        h = jnp.einsum('bsh,bha->bsa', hidden_states, w1) + b1[language_ids][:, None, :]
        h = jax.nn.relu(h)
        adapted = jnp.einsum('bsa,bah->bsh', h, w2) + b2[language_ids][:, None, :]
        x = hidden_states + adapted
        mean = jnp.mean(x, axis=-1, keepdims=True)
        var = jnp.mean(jnp.square(x - mean), axis=-1, keepdims=True)
        normed = (x - mean) * jax.lax.rsqrt(var + LN_EPS)
        return normed * gamma[language_ids][:, None, :] + beta[language_ids][:, None, :]
    x = x + _L0_cond_ref(x, L0_cond_tau_ctx, condB_tauraws, L0_cond_Wg, L0_cond_bg, L0_cond_Wn1, L0_cond_bn1, cond_256, condB_bn2, cond_1024, L0_cond_Wsoma, L0_cond_bsoma, L0_cond_Wtemp, L0_cond_btemp, L0_cond_Wout, L0_cond_gamma, L0_cond_beta)
    x = x + _L1_cond_ref(x, itok_B_0_8, L1_cond_W1, L1_cond_b1, L1_cond_W2, L1_cond_b2, L1_cond_gamma, L1_cond_beta)
    return x

_drawn_inputs = setup_inputs


def setup_inputs(seed=0):
    import zlib

    import numpy as np

    out = dict(_drawn_inputs(seed))
    spreads = {'condB_bn2': (0.0, 2.0),
     'L0_cond_bg': (-0.5, 0.6),
     'L0_cond_bn1': (0.0, 2.0),
     'L0_cond_bsoma': (0.0, 0.1),
     'L0_cond_btemp': (0.0, 0.267),
     'L0_cond_gamma': (1.0, 0.2),
     'L0_cond_beta': (0.0, 0.1),
     'L1_cond_b1': (0.0, 0.463),
     'L1_cond_b2': (0.0, 0.318),
     'L1_cond_gamma': (1.0, 0.2),
     'L1_cond_beta': (0.0, 0.1)}
    factors = {'condB_tauraws': 8.0, 'cond_256': 64.0, 'cond_1024': 189.311, 'L0_cond_Wn1': 191.91}
    for name, (base, spread) in spreads.items():
        noise = np.random.default_rng([zlib.crc32(name.encode()), seed]).standard_normal(out[name].shape)
        drawn = base * np.exp(spread * noise) if base else spread * noise
        out[name] = jnp.asarray(drawn.astype(out[name].dtype))
    for name, factor in factors.items():
        out[name] = (out[name] * factor).astype(out[name].dtype)
    return out
```

```python
from contextlib import ExitStack

import concourse.bass as bass
from concourse import mybir

F32 = mybir.dt.float32
I32 = mybir.dt.int32
ALU = mybir.AluOpType
ACT = mybir.ActivationFunctionType
AX = mybir.AxisListType

P = 128
B, T, E, D = 128, 64, 256, 128
H = 64
L = 16
NK = T // L
SEQ = 8
TOK = SEQ * T
TILES = B // SEQ
PAIRS = SEQ // 2
EH = E // P
LAGS = L // 2 + 1
EPS = 1e-5
RING = 4


class Pass:

    def __init__(self, n, par, half, act_before, dve_before, phases=None, heavy=True, tail=True, front=True):
        self.n, self.par, self.heavy, self.tail, self.front = n, par, heavy, tail, front
        self.tail_loads = half + par
        a, v = [], []
        if tail:
            a += [("temp", e) for e in range(EH)]
        if front:
            a += [("wg", e) for e in range(EH)] + [("n1", 0)] + [("soma", e) for e in range(EH)]
        if tail:
            a += [("yT", e) for e in range(EH)]
        if front:
            a += [("n2", 0)]
        if tail:
            a += [("w1", 0)]
        if front:
            a += [("gnat", s) for s in range(2)]
        if heavy:
            a += [("carry", k) for k in range(1, NK)]
            v += [("lag0", j) for j in range(6)]
        if tail:
            v += [("out", s) for s in range(2)]
        if heavy:
            v += [("lag0", j) for j in range(6, LAGS)] + [("lag1", j) for j in range(6)]
        if front:
            v += [("modnat", 0)]
        if heavy:
            v += [("lag1", j) for j in range(6, LAGS)]
        if tail:
            v += [("w2", s) for s in range(2)]
        if heavy:
            v += [(f"state{k}", p) for k in range(1, NK) for p in range(PAIRS)]
            v += [("carryT", k) for k in range(1, NK)]
        self.a_order, self.v_order = a, v
        self.a0, self.v0 = act_before, dve_before
        self.phases = phases or (act_before % RING, dve_before % RING)

    def act(self, name, k=0):
        return self.a0 + self.a_order.index((name, k))

    def dve(self, name, k=0):
        return self.v0 + self.v_order.index((name, k))

    def act_bank(self, banks, name, k=0):
        return banks[(self.phases[0] + self.a_order.index((name, k))) % RING]

    def dve_bank(self, banks, name, k=0):
        return banks[(self.phases[1] + self.v_order.index((name, k))) % RING]

    def next_act(self):
        return self.a0 + len(self.a_order)

    def next_dve(self):
        return self.v0 + len(self.v_order)


FILL = Pass(-1, 1, -1, 0, 0, heavy=False, tail=False)
FIRST = Pass(0, 0, 0, FILL.next_act(), FILL.next_dve(), tail=False)
SECOND = FULL = Pass(1, 1, 0, FIRST.next_act(), FIRST.next_dve())
FULL_ACT, FULL_DVE = len(FULL.a_order), len(FULL.v_order)
assert 2 * FULL_ACT % RING == 0 and 2 * FULL_DVE % RING == 0


def loop_pass(j, u):
    a, v = SECOND.next_act() + FULL_ACT * u, SECOND.next_dve() + FULL_DVE * u
    return Pass(2 * j + u + 2, u, j + 1, 2 * FULL_ACT * j + a, 2 * FULL_DVE * j + v, (a % RING, v % RING))


LOOPS = (TILES - 4) // 2
SECOND_LAST = Pass(TILES - 2, 0, TILES // 2 - 1, FULL.a0 + FULL_ACT * (TILES - 3), FULL.v0 + FULL_DVE * (TILES - 3))
LAST = Pass(TILES - 1, 1, TILES // 2 - 1, SECOND_LAST.next_act(), SECOND_LAST.next_dve(), front=False)
DRAIN = Pass(TILES, 0, TILES // 2, LAST.next_act(), LAST.next_dve(), heavy=False, front=False)

POOL_ALL = 7
PE_TURNS, PE_ALL = EH + NK, EH + NK + EH
ACT_ALL = 2 + (NK - 1) + 1 + EH
DVE_TABLES, DVE_MAX, DVE_SOFTMAX, DVE_ALL = 32, 34, 37, 53


def prod_slot(e, j):
    return (e * (LAGS - 1) + j - 1) % PRODS


PRODS = 4


def build(nc, xT_d, x_d, tau_d, wn2T_d, bn2_d, blend_d, ids_d, tauc_d, wgT_d, bg_d, wn1T_d, bn1_d,
          wsT_d, bs_d, wtT_d, bt_d, woT_d, gamma_d, beta_d, w1_d, b1_d, w2_d, rows_d, out_d):
    NL = w1_d.shape[0]
    ctx = ExitStack()
    with ctx:
        def sb(name, shape, dt=F32):
            return ctx.enter_context(nc.sbuf_tensor(name, shape, dt))

        def sem(name):
            return ctx.enter_context(nc.semaphore(name))

        ident = sb("ident", [P, P])
        wg = sb("wg", [P, 2 * EH, E])
        wn1 = sb("wn1", [P, EH, H])
        wn2 = sb("wn2", [H, D])
        ws = sb("ws", [P, EH, E])
        wt = sb("wt", [P, EH, E])
        wo = sb("wo", [P, EH, E])
        cols = sb("cols", [P, 10])
        bgc, bsc, btc = (cols[:, 2 * i:2 * i + 2] for i in range(3))
        bn1c, bn2c = cols[0:H, 6:7], cols[:, 7:8]
        tauc = cols[:, 8:9]
        taud = cols[:, 9:10]
        alpha = sb("alpha", [P, 2])
        gam0 = sb("gam0", [P, E])
        bet0 = sb("bet0", [P, E])
        lagw = sb("lagw", [P, L, E])
        bw = lagw[:, 0, :]
        revpow = sb("revpow", [P, T])
        powsq = sb("powsq", [P, 8])
        carrypow = sb("carrypow", [P, 3 * L])
        statepow = sb("statepow", [P, NK - 1, D])
        decay = sb("decay", [P, TOK])
        ids = sb("ids", [1, B], I32)
        ids_l = sb("ids_l", [NL, B], I32)
        lang_i = sb("lang_i", [NL, 1], I32)
        lang = sb("lang", [NL, 1])
        idf = sb("idf", [NL, B])
        onehot = sb("onehot", [NL, B])
        b1d = sb("b1d", [NL, 2 * H])
        b1g = sb("b1g", [P, B])
        smax = sb("smax", [P, EH])
        ssum = sb("ssum", [P, EH])
        srec = sb("srec", [P, EH])
        waited = sb("waited", [1, 1])
        minus_half = sb("minus_half", [P, PAIRS])

        xT = sb("xT", [P, EH, TOK])
        xn = sb("xn", [P, PAIRS, E])
        rows = [sb(f"rows{i}", [P, PAIRS, 3, E]) for i in range(2)]
        w1 = [sb(f"w1_{i}", [P, PAIRS, EH, 2 * H]) for i in range(2)]
        w2 = [sb(f"w2_{i}", [P, PAIRS, E]) for i in range(2)]
        ctxT = sb("ctxT", [P, EH, TOK])
        wgT = sb("wgT", [P, EH, TOK])
        h1 = sb("h1", [H, TOK])
        sig = sb("sig", [P, TOK])
        soma = [sb(f"soma{i}", [P, EH, TOK]) for i in range(2)]
        g = [sb(f"g{i}", [P, EH, SEQ, T]) for i in range(2)]
        mod = [sb(f"mod{i}", [P, SEQ, T]) for i in range(2)]
        temporal = [sb(f"temporal{i}", [P, EH, SEQ, T]) for i in range(2)]
        gnat = [sb(f"gnat{i}", [P, PAIRS, 2, E]) for i in range(2)]
        decmod = [sb(f"decmod{i}", [P, PAIRS, NK - 1, D]) for i in range(2)]
        prod = sb("prod", [P, PRODS, TOK])
        statepow_t = prod[:, 0, 0:(NK - 1) * P].rearrange("d (k t) -> d k t", t=P)
        state = sb("state", [P, 2, PAIRS, 2 * E])
        carry = sb("carry", [P, NK, E])
        gate = sb("gate", [P, EH, TOK])
        gs = sb("gs", [P, EH, TOK])
        y = sb("y", [P, PAIRS, E])
        z = sb("z", [P, PAIRS, E])
        yT = gs
        hid = sb("hid", [P, PAIRS, P])
        stats = sb("stats", [P, PAIRS, 6])
        mv = sb("mv", [P, PAIRS, 2])
        ve = sb("ve", [P, PAIRS])
        rstd = sb("rstd", [P, PAIRS])
        stats2 = sb("stats2", [P, PAIRS, 6])
        mv2 = sb("mv2", [P, PAIRS, 2])
        ve2 = sb("ve2", [P, PAIRS])
        rstd2 = sb("rstd2", [P, PAIRS])

        abank = [ctx.enter_context(nc.psum_tensor(f"abank{i}", [P, 512], F32)) for i in range(RING)]
        vbank = [ctx.enter_context(nc.psum_tensor(f"vbank{i}", [P, 512], F32)) for i in range(RING)]

        act_filled = sem("act_filled")
        act_taken = sem("act_taken")
        dve_filled = sem("dve_filled")
        dve_taken = sem("dve_taken")
        const_loaded = sem("const_loaded")
        ids_loaded = sem("ids_loaded")
        pool_const = sem("pool_const")
        dve_const = sem("dve_const")
        act_const = sem("act_const")
        pe_const = sem("pe_const")
        xT_loaded = sem("xT_loaded")
        xn_loaded = sem("xn_loaded")
        rows_loaded = [sem(f"rows_loaded{i}") for i in range(2)]
        w1_loaded = [sem(f"w1_loaded{i}") for i in range(2)]
        w2_loaded = [sem(f"w2_loaded{i}") for i in range(2)]
        ctx_ready = sem("ctx_ready")
        g_ready = sem("g_ready")
        gs_ready = sem("gs_ready")
        mod_ready = sem("mod_ready")
        lags_added = sem("lags_added")
        xbeta_ready = sem("xbeta_ready")
        stats_done = sem("stats_done")
        rstd_ready = sem("rstd_ready")
        y_ready = sem("y_ready")
        yb_ready = sem("yb_ready")
        stats2_done = sem("stats2_done")
        rstd2_ready = sem("rstd2_ready")
        out_ready = sem("out_ready")
        stored = sem("stored")

        LAG_ADDS = 2 * (2 * (LAGS - 2) + 1)

        def by_chunk_step(ap):
            return ap.rearrange("c (b p k) -> c b k p", b=SEQ, k=NK)

        def in_time(ap):
            return ap.rearrange("c (b k p) -> c b k p", b=SEQ, k=NK)

        def pair_rows(dram, n):
            return dram[bass.ds(n * TOK, TOK), :].rearrange("(p t) c -> t p c", p=PAIRS)

        block = ctx.enter_context(nc.Block())

        CONST_LOADS = 22

        @block.sync
        def _(sp):
            def load_xT(n):
                sp.dma_start(xT[:], xT_d[:, bass.ds(n * TOK, TOK)].rearrange("(k p) t -> p k t", p=P))\
                    .then_inc(xT_loaded, 16)

            def load_adapters(n, par):
                for q in range(SEQ):
                    lang_q = sp.value_load(ids[0:1, bass.ds(n * SEQ + q, 1)], min_val=0, max_val=NL - 1)
                    half = slice((q % 2) * T, (q % 2 + 1) * T)
                    sp.dma_start(w1[par][:, q // 2, :, (q % 2) * H:(q % 2 + 1) * H], w1_d[bass.ds(lang_q, 1), :, :].rearrange("l (k c) a -> c (l k) a", k=EH))\
                        .then_inc(w1_loaded[par], 16)
                    sp.dma_start(w2[par][half, q // 2, :], w2_d[bass.ds(lang_q, 1), :, :].rearrange("l a c -> (l a) c"))\
                        .then_inc(w2_loaded[par], 16)
                    sp.dma_start(rows[par][half, q // 2, :, :].rearrange("t r c -> t (r c)"),
                                 rows_d[bass.ds(lang_q, 1), :].to_broadcast([T, 3 * E]))\
                        .then_inc(rows_loaded[par], 16)

            sp.dma_start(ids[:], ids_d).then_inc(ids_loaded, 16)
            sp.dma_start(taud, tau_d.rearrange("(d a) -> d a", a=1)).then_inc(const_loaded, 16)
            sp.dma_start(tauc, tauc_d.to_broadcast([P, 1])).then_inc(const_loaded, 16)
            load_xT(0)
            for w, src in ((wg, wgT_d), (wn1, wn1T_d), (ws, wsT_d), (wt, wtT_d), (wo, woT_d)):
                sp.dma_start(w[:], src.rearrange("(k c) e -> c k e", c=P)).then_inc(const_loaded, 16)
            sp.dma_start(wn2[:], wn2T_d).then_inc(const_loaded, 16)
            sp.dma_start(bw, blend_d).then_inc(const_loaded, 16)
            for c, src in ((bgc, bg_d), (bsc, bs_d), (btc, bt_d)):
                for e in range(EH):
                    sp.dma_start(c[:, e:e + 1], src[e * P:(e + 1) * P].rearrange("(p a) -> p a", a=1))\
                        .then_inc(const_loaded, 16)
            sp.dma_start(bn1c, bn1_d.rearrange("(p a) -> p a", a=1)).then_inc(const_loaded, 16)
            sp.dma_start(bn2c, bn2_d.rearrange("(p a) -> p a", a=1)).then_inc(const_loaded, 16)
            sp.dma_start(gam0[:], gamma_d.rearrange("(a c) -> a c", a=1).to_broadcast([P, E])).then_inc(const_loaded, 16)
            sp.dma_start(bet0[:], beta_d.rearrange("(a c) -> a c", a=1).to_broadcast([P, E])).then_inc(const_loaded, 16)
            sp.dma_start(ids_l[:], ids_d.to_broadcast([NL, B])).then_inc(const_loaded, 16)
            for h in range(2):
                sp.dma_start(b1d[:, h * H:(h + 1) * H], b1_d).then_inc(const_loaded, 16)
            sp.wait_ge(ids_loaded, 16)

            def one_pass(s):
                n, par = s.n, s.par
                if s.tail:
                    sp.wait_ge(y_ready, PAIRS * (n - 1))
                    sp.dma_start(xn[:], pair_rows(x_d, n - 1)).then_inc(xn_loaded, 16)
                if s.front:
                    sp.wait_ge(act_taken, s.a0)
                    sp.wait_ge(g_ready, EH * (n + 1))
                    load_xT(n + 1)
                if s.heavy:
                    load_adapters(n, par)
                if s.tail:
                    sp.wait_ge(out_ready, PAIRS * n)
                    sp.dma_start(pair_rows(out_d, n - 1), z[:]).then_inc(stored, 16)

            one_pass(FIRST)
            one_pass(SECOND)
            with sp.Fori(0, LOOPS) as j:
                for u in range(2):
                    one_pass(loop_pass(j, u))
            one_pass(SECOND_LAST)
            one_pass(LAST)
            one_pass(DRAIN)
            sp.wait_ge(stored, 16 * TILES)

        @block.tensor
        def _(pe):
            def fill_act(use):
                if not isinstance(use, int) or use >= RING:
                    pe.wait_ge(act_taken, use - (RING - 1))

            def fill_dve(use):
                if not isinstance(use, int) or use >= RING:
                    pe.wait_ge(dve_taken, use - (RING - 1))

            def a_bank(s, name, k=0):
                return s.act_bank(abank, name, k)

            def v_bank(s, name, k=0):
                return s.dve_bank(vbank, name, k)

            def dense(bank, w, srcs, e, width=P, m=P):
                for i, (k, src) in enumerate(srcs):
                    last = pe.matmul(bank[0:m, :], w[:, k, e * P:e * P + width], src,
                                     start=(i == 0), stop=(i == len(srcs) - 1))
                return last

            def lag_bank(s, e, j):
                name = f"lag{e}"
                fill_dve(s.dve(name, j))
                bank = v_bank(s, name, j)[:].rearrange("c (b t) -> c b t", b=SEQ)
                m = mod[s.par]
                last = pe.matmul(bank[:, :, NK * j:T], lagw[:, j, e * P:(e + 1) * P], m[:, :, 0:NK * (L - j)],
                                 start=True, stop=True)
                if 0 < j < L // 2:
                    last = pe.matmul(bank[:, :, 0:NK * j], lagw[:, L - j, e * P:(e + 1) * P], m[:, :, 0:NK * j],
                                     start=True, stop=True)
                last.then_inc(dve_filled, 1)

            def front_gates(s):
                x, f = xT, s.n + 1
                pe.wait_ge(xT_loaded, 16 * (s.n + 2))
                pe.wait_ge(ctx_ready, 2 * f + 2)
                for e in range(EH):
                    fill_act(s.act("wg", e))
                    dense(a_bank(s, "wg", e), wg, [(0, x[:, 0, :]), (1, x[:, 1, :]), (2, ctxT[:, 0, :]),
                                                  (3, ctxT[:, 1, :])], e).then_inc(act_filled, 1)
                fill_act(s.act("n1"))
                dense(a_bank(s, "n1"), wn1, [(0, x[:, 0, :]), (1, x[:, 1, :])], 0, H, H).then_inc(act_filled, 1)
                for e in range(EH):
                    fill_act(s.act("soma", e))
                    dense(a_bank(s, "soma", e), ws, [(0, x[:, 0, :]), (1, x[:, 1, :])], e).then_inc(act_filled, 1)

            def front_mod(s):
                pe.wait_ge(act_taken, s.act("n1") + 1)
                fill_act(s.act("n2"))
                pe.matmul(a_bank(s, "n2")[:], wn2[:], h1[:], start=True, stop=True).then_inc(act_filled, 1)

            def front_transposes(s):
                f = s.n + 1
                pe.wait_ge(g_ready, EH * (f + 1))
                for h in range(2):
                    fill_act(s.act("gnat", h))
                    for i in range(2):
                        p = 2 * h + i
                        for e in range(EH):
                            last = pe.transpose(a_bank(s, "gnat", h)[:, i * E + e * P:i * E + (e + 1) * P],
                                                g[1 - s.par][:, e, 2 * p:2 * p + 2, :].rearrange("c b t -> c (b t)"), ident[:])
                    last.then_inc(act_filled, 1)
                pe.wait_ge(mod_ready, f + 1)
                fill_dve(s.dve("modnat"))
                for p in range(PAIRS):
                    last = pe.transpose(v_bank(s, "modnat")[:, p * D:(p + 1) * D],
                                        mod[1 - s.par][:, 2 * p:2 * p + 2, :].rearrange("d b t -> d (b t)"), ident[:])
                last.then_inc(dve_filled, 1)

            def tail_temporal(s):
                pe.wait_ge(dve_taken, s.v0)
                for e in range(EH):
                    fill_act(s.act("temp", e))
                    src = temporal[1 - s.par]
                    dense(a_bank(s, "temp", e), wt, [(k, src[:, k, :, :].rearrange("c b t -> c (b t)")) for k in range(EH)], e)\
                        .then_inc(act_filled, 1)

            def tail_out(s):
                pe.wait_ge(gs_ready, EH * s.n)
                for h in range(2):
                    fill_dve(s.dve("out", h))
                    for i in range(2):
                        p = 2 * h + i
                        for k in range(EH):
                            last = pe.matmul(v_bank(s, "out", h)[:, i * E:(i + 1) * E], gs[:, k, p * P:(p + 1) * P],
                                             wo[:, k, :], start=(k == 0), stop=(k == EH - 1))
                    last.then_inc(dve_filled, 1)

            def tail_yT(s):
                pe.wait_ge(y_ready, PAIRS * s.n)
                for e in range(EH):
                    fill_act(s.act("yT", e))
                    for p in range(PAIRS):
                        last = pe.transpose(a_bank(s, "yT", e)[:, p * P:(p + 1) * P], y[:, p, e * P:(e + 1) * P], ident[:])
                    last.then_inc(act_filled, 1)

            def tail_w1(s):
                pe.wait_ge(act_taken, s.act("yT", 1) + 1)
                pe.wait_ge(w1_loaded[1 - s.par], 16 * SEQ * s.tail_loads)
                fill_act(s.act("w1"))
                for p in range(PAIRS):
                    for k in range(EH):
                        last = pe.matmul(a_bank(s, "w1")[:, p * P:(p + 1) * P], w1[1 - s.par][:, p, k, :],
                                         yT[:, k, p * P:(p + 1) * P], start=(k == 0), stop=(k == EH - 1))
                last.then_inc(act_filled, 1)

            def tail_w2(s):
                pe.wait_ge(act_taken, s.act("w1") + 1)
                pe.wait_ge(w2_loaded[1 - s.par], 16 * SEQ * s.tail_loads)
                for h in range(2):
                    fill_dve(s.dve("w2", h))
                    for i in range(2):
                        p = 2 * h + i
                        last = pe.matmul(v_bank(s, "w2", h)[:, i * E:(i + 1) * E], hid[:, p, :], w2[1 - s.par][:, p, :],
                                         start=True, stop=True)
                    last.then_inc(dve_filled, 1)

            def states(s, k):
                for p in range(PAIRS):
                    fill_dve(s.dve(f"state{k}", p))
                    pe.matmul(v_bank(s, f"state{k}", p)[:], decmod[s.par][:, p, k - 1, :],
                              gnat[s.par][:, p, :, :].rearrange("t b c -> t (b c)"), start=True, stop=True)\
                        .then_inc(dve_filled, 1)

            def carried(s, k):
                fill_act(s.act("carry", k))
                pe.wait_ge(dve_taken, s.dve(f"state{k}", PAIRS - 1) + 1)
                bank = a_bank(s, "carry", k)
                for b in range(2):
                    for p in range(PAIRS):
                        last = pe.matmul(bank[2 * L * p:2 * L * (p + 1), 0:E], carrypow[:, L * (1 - b):L * (3 - b)],
                                         state[:, k % 2, p, b * E:(b + 1) * E], start=(b == 0), stop=(b == 1))
                last.then_inc(act_filled, 1)

            def carried_T(s, k):
                pe.wait_ge(act_taken, s.act("carry", k) + 1)
                fill_dve(s.dve("carryT", k))
                for e in range(EH):
                    last = pe.transpose(v_bank(s, "carryT", k)[:, e * P:(e + 1) * P], carry[:, k, e * P:(e + 1) * P], ident[:])
                last.then_inc(dve_filled, 1)

            def one_pass(s):
                def lags(e, j0, j1):
                    if s.heavy:
                        for j in range(j0, j1):
                            lag_bank(s, e, j)
                if s.heavy:
                    pe.wait_ge(mod_ready, s.n + 1)
                lags(0, 0, 3)
                if s.tail:
                    tail_temporal(s)
                lags(0, 3, 6)
                if s.tail:
                    tail_out(s)
                lags(0, 6, LAGS)
                if s.front:
                    front_gates(s)
                lags(1, 0, 3)
                if s.tail:
                    tail_yT(s)
                if s.front:
                    front_mod(s)
                lags(1, 3, 6)
                if s.tail:
                    tail_w1(s)
                if s.front:
                    front_transposes(s)
                lags(1, 6, LAGS)
                if s.tail:
                    tail_w2(s)
                if s.heavy:
                    states(s, 1)
                    states(s, 2)
                    carried(s, 1)
                    states(s, 3)
                    carried(s, 2)
                    carried(s, 3)
                    for k in range(1, NK):
                        carried_T(s, k)

            pe.wait_ge(pool_const, 2)
            pe.wait_ge(const_loaded, 16 * CONST_LOADS)
            for e in range(EH):
                pe.transpose(abank[0][:, e * P:(e + 1) * P], bw[:, e * P:(e + 1) * P], ident[:]).then_inc(pe_const, 1)
            pe.wait_ge(dve_const, DVE_TABLES)
            for k in range(1, NK):
                pe.transpose(abank[1][:, (k - 1) * P:k * P], statepow_t[:, k - 1, :], ident[:]).then_inc(pe_const, 1)
            pe.matmul(abank[2][:, 0:B], b1d[:], onehot[:], start=True, stop=True).then_inc(pe_const, 1)
            pe.wait_ge(dve_const, DVE_SOFTMAX)
            for e in range(EH):
                pe.transpose(abank[3][:, e * P:(e + 1) * P], soma[0][:, e, 0:P], ident[:]).then_inc(pe_const, 1)
            pe.wait_ge(dve_const, DVE_ALL)
            pe.wait_ge(act_const, ACT_ALL)
            one_pass(FILL)
            one_pass(FIRST)
            one_pass(SECOND)
            with pe.Fori(0, LOOPS) as j:
                for u in range(2):
                    one_pass(loop_pass(j, u))
            one_pass(SECOND_LAST)
            one_pass(LAST)
            one_pass(DRAIN)

        @block.scalar
        def _(act):
            def a_bank(s, name, k=0):
                return s.act_bank(abank, name, k)

            def temporal_gate(s):
                act.wait_ge(gs_ready, EH * (s.n - 1))
                for e in range(EH):
                    act.wait_ge(act_filled, s.act("temp", e) + 1)
                    act.activation(in_time(gate[:, e, :]), by_chunk_step(a_bank(s, "temp", e)[:]),
                                   ACT.Sigmoid, bias=btc[:, e:e + 1]).then_inc(act_taken, 1)

            def front_gates(s):
                f = s.n + 1
                if s is not FILL:
                    act.wait_ge(g_ready, EH * f)
                for e in range(EH):
                    act.wait_ge(act_filled, s.act("wg", e) + 1)
                    act.activation(by_chunk_step(wgT[:, e, :]), in_time(a_bank(s, "wg", e)[:]), ACT.Sigmoid, bias=bgc[:, e:e + 1])\
                        .then_inc(act_taken, 1)
                act.wait_ge(act_filled, s.act("n1") + 1)
                act.activation(h1[:], a_bank(s, "n1")[0:H, :], ACT.Gelu, bias=bn1c).then_inc(act_taken, 1)
                if s.tail:
                    act.wait_ge(gs_ready, EH * s.n)
                for e in range(EH):
                    act.wait_ge(act_filled, s.act("soma", e) + 1)
                    act.activation(soma[1 - s.par][:, e, :], a_bank(s, "soma", e)[:], ACT.Gelu, bias=bsc[:, e:e + 1])\
                        .then_inc(act_taken, 1)

            def y_turned(s):
                for e in range(EH):
                    act.wait_ge(act_filled, s.act("yT", e) + 1)
                    act.activation(yT[:, e, :], a_bank(s, "yT", e)[:], ACT.Copy).then_inc(act_taken, 1)

            def front_mod(s):
                if s is not FILL:
                    act.wait_ge(mod_ready, s.n + 1)
                act.wait_ge(act_filled, s.act("n2") + 1)
                act.activation(by_chunk_step(sig[:]), in_time(a_bank(s, "n2")[:]), ACT.Sigmoid, bias=bn2c).then_inc(act_taken, 1)

            def adapter_hidden(s):
                m = s.n - 1
                act.wait_ge(dve_filled, s.v0)
                act.wait_ge(act_filled, s.act("w1") + 1)
                for p in range(PAIRS):
                    for b in range(2):
                        half = slice(b * H, (b + 1) * H)
                        i = act.activation(hid[half, p, b * T:(b + 1) * T],
                                           a_bank(s, "w1")[half, p * P + b * T:p * P + (b + 1) * T], ACT.Relu,
                                           bias=b1g[half, bass.ds(m * SEQ + 2 * p + b, 1)])
                i.then_inc(act_taken, 1)

            def g_by_token(s):
                if s.heavy and s.tail:
                    act.wait_ge(dve_filled, s.v0)
                for h in range(2):
                    act.wait_ge(act_filled, s.act("gnat", h) + 1)
                    bank = a_bank(s, "gnat", h)[:].rearrange("t (i c) -> t i c", i=2)
                    for b in range(2):
                        half = slice(b * T, (b + 1) * T)
                        i = act.activation(gnat[1 - s.par][half, 2 * h:2 * h + 2, b, :], bank[half, :, :], ACT.Copy)
                    i.then_inc(act_taken, 1)

            def carried(s):
                if s is not FIRST:
                    act.wait_ge(dve_filled, s.v0)
                for k in range(1, NK):
                    act.wait_ge(act_filled, s.act("carry", k) + 1)
                    act.activation(carry[:, k, :], a_bank(s, "carry", k)[:, 0:E], ACT.Copy).then_inc(act_taken, 1)

            def one_pass(s):
                if s.tail:
                    temporal_gate(s)
                if s.front:
                    front_gates(s)
                if s.tail:
                    y_turned(s)
                if s.front:
                    front_mod(s)
                if s.tail:
                    adapter_hidden(s)
                if s.front:
                    g_by_token(s)
                if s.heavy:
                    carried(s)

            act.wait_ge(const_loaded, 16 * CONST_LOADS)
            act.activation(alpha[:, 0:1], taud, ACT.Sigmoid, scale=-1.0).then_inc(act_const, 1)
            act.activation(alpha[:, 1:2], tauc, ACT.Sigmoid, scale=-1.0).then_inc(act_const, 1)
            act.wait_ge(pe_const, 2 + NK - 1)
            for k in range(1, NK):
                act.activation(statepow[:, k - 1, :], abank[1][:, (k - 1) * P:k * P], ACT.Copy).then_inc(act_const, 1)
            act.wait_ge(pe_const, 2 + NK)
            act.activation(b1g[:], abank[2][:, 0:B], ACT.Copy).then_inc(act_const, 1)
            act.wait_ge(dve_const, DVE_MAX)
            for e in range(EH):
                act.activation(soma[1][:, e, 0:P], abank[0][:, e * P:(e + 1) * P], ACT.Exp, bias=smax[:, e:e + 1],
                               accum_out=ssum[:, e:e + 1]).then_inc(act_const, 1)
            act.wait_ge(pool_const, POOL_ALL)
            act.wait_ge(dve_const, DVE_ALL)
            one_pass(FILL)
            one_pass(FIRST)
            one_pass(SECOND)
            with act.Fori(0, LOOPS) as j:
                for u in range(2):
                    one_pass(loop_pass(j, u))
            one_pass(SECOND_LAST)
            one_pass(LAST)
            one_pass(DRAIN)

        @block.gpsimd
        def _(pool):
            def x_plus_beta(s):
                m = s.n - 1
                pool.wait_ge(xn_loaded, 16 * s.n)
                pool.wait_ge(y_ready, PAIRS * m)
                pool.tensor_tensor(xn[:], xn[:], bet0[:, None, :].to_broadcast([P, PAIRS, E]), ALU.add)\
                    .then_inc(xbeta_ready, 1)

            def add_lags(s, e, j0, j1):
                base = LAG_ADDS * s.n
                dst, t0 = temporal[s.par], e * (LAG_ADDS // 2)
                for j in range(max(j0, 1), j1):
                    slot = prod[:, prod_slot(e, j), :].rearrange("c (b t) -> c b t", b=SEQ)
                    pool.wait_ge(dve_taken, s.dve(f"lag{e}", j) + 1)
                    parts = [(dst[:, e, :, NK * j:T], slot[:, :, NK * j:T])]
                    if j < L // 2:
                        parts.append((dst[:, e, :, NK * (L - j):T], slot[:, :, 0:NK * j]))
                    for i, (to, frm) in enumerate(parts):
                        done = t0 + 2 * (j - 1) + i
                        if j > 1 or i or e:
                            pool.wait_ge(lags_added, base + done)
                        pool.tensor_tensor(to, to, frm, ALU.add).then_inc(lags_added, 1)

            def rstds(s, ve_, rstd_, done, steps, ready):
                m = s.n - 1
                for h in range(2):
                    pool.wait_ge(done, 2 * steps * m + steps * (h + 1))
                    pool.tensor_tensor(rstd_[:, 2 * h:2 * h + 2], ve_[:, 2 * h:2 * h + 2], minus_half[:, 0:2], ALU.pow)\
                        .then_inc(ready, 1)

            def y_sums(s):
                m = s.n - 1
                r = rows[1 - s.par]
                pool.wait_ge(rows_loaded[1 - s.par], 16 * SEQ * s.tail_loads)
                pool.wait_ge(y_ready, PAIRS * s.n)
                pool.tensor_tensor(r[:, :, 0, :], y[:], r[:, :, 0, :], ALU.add).then_inc(yb_ready, 1)
                pool.tensor_tensor(r[:, :, 2, :], y[:], r[:, :, 2, :], ALU.add).then_inc(yb_ready, 1)

            def one_pass(s):
                if s.heavy:
                    add_lags(s, 0, 0, 6)
                if s.tail:
                    x_plus_beta(s)
                    rstds(s, ve, rstd, stats_done, 5, rstd_ready)
                if s.heavy:
                    add_lags(s, 0, 6, LAGS)
                if s.tail:
                    y_sums(s)
                if s.heavy:
                    add_lags(s, 1, 0, 3)
                if s.heavy:
                    add_lags(s, 1, 3, LAGS)
                if s.tail:
                    rstds(s, ve2, rstd2, stats2_done, 7, rstd2_ready)

            pool.memset(ident[:], 0.0).then_inc(pool_const, 1)
            pool.wait_ge(pool_const, 1)
            pool.affine_select(out=ident[:], in_=ident[:], compare_op=ALU.not_equal, fill=1.0, base=0,
                               pattern=[[-1, P]], channel_multiplier=1).then_inc(pool_const, 1)
            pool.iota(lang_i[:], pattern=[[0, 1]], base=0, channel_multiplier=1).then_inc(pool_const, 1)
            for buf in (*gnat, hid, minus_half):
                pool.memset(buf[:], 0.0 if buf is not minus_half else -0.5).then_inc(pool_const, 1)
            pool.wait_ge(const_loaded, 16 * CONST_LOADS)
            pool.wait_ge(pool_const, POOL_ALL)
            one_pass(FILL)
            one_pass(FIRST)
            one_pass(SECOND)
            with pool.Fori(0, LOOPS) as j:
                for u in range(2):
                    one_pass(loop_pass(j, u))
            one_pass(SECOND_LAST)
            one_pass(LAST)
            one_pass(DRAIN)

        @block.vector
        def _(dve):
            def v_bank(s, name, k=0):
                return s.dve_bank(vbank, name, k)

            def context(s):
                dve.wait_ge(xT_loaded, 16 * (s.n + 2))
                for e in range(EH):
                    dve.tensor_tensor_scan(ctxT[:, e, :], decay[:], xT[:, e, :], 0.0, ALU.mult, ALU.add)\
                        .then_inc(ctx_ready, 1)

            def lag_products(s, e, j0, j1):
                for j in range(j0, j1):
                    name = f"lag{e}"
                    dve.wait_ge(dve_filled, s.dve(name, j) + 1)
                    bank = v_bank(s, name, j)[:].rearrange("c (b t) -> c b t", b=SEQ)
                    if j == 0:
                        to = temporal[s.par][:, e, :, :]
                    else:
                        to = prod[:, prod_slot(e, j), :].rearrange("c (b t) -> c b t", b=SEQ)
                        prod_free(s, e, j)
                    last = dve.tensor_tensor(to[:, :, NK * j:T], bank[:, :, NK * j:T], g[s.par][:, e, :, 0:T - NK * j], ALU.mult)
                    if 0 < j < L // 2:
                        last = dve.tensor_tensor(to[:, :, 0:NK * j], bank[:, :, 0:NK * j], g[s.par][:, e, :, 0:NK * j], ALU.mult)
                    last.then_inc(dve_taken, 1)

            def prod_free(s, e, j):
                i = e * (LAGS - 1) + j - 1 - PRODS
                before, i = (i < 0), i % (2 * (LAGS - 1))
                ei, ji = i // (LAGS - 1), i % (LAGS - 1) + 1
                if before and s is FIRST:
                    return
                adds = ei * (LAG_ADDS // 2) + min(2 * ji, LAG_ADDS // 2)
                dve.wait_ge(lags_added, LAG_ADDS * (s.n - before) + adds)

            def gated_soma(s):
                for e in range(EH):
                    dve.wait_ge(act_taken, s.act("temp", e) + 1)
                    dve.tensor_tensor(gs[:, e, :], gate[:, e, :], soma[1 - s.par][:, e, :], ALU.mult).then_inc(gs_ready, 1)

            def gated_x(s):
                for e in range(EH):
                    dve.wait_ge(act_taken, s.act("wg", e) + 1)
                    dve.tensor_tensor(by_chunk_step(g[1 - s.par][:, e, :, :].rearrange("c b t -> c (b t)")),
                                      in_time(xT[:, e, :]), by_chunk_step(wgT[:, e, :]), ALU.mult).then_inc(g_ready, 1)

            def front_mod(s):
                dve.wait_ge(act_taken, s.act("n2") + 1)
                dve.tensor_scalar(mod[1 - s.par][:].rearrange("d b t -> d (b t)"), sig[:], 0.5, None, ALU.add)\
                    .then_inc(mod_ready, 1)

            def decayed_mod(s):
                dve.wait_ge(dve_filled, s.dve("modnat") + 1)
                bank = v_bank(s, "modnat")
                for p in range(PAIRS):
                    i = dve.tensor_tensor(decmod[1 - s.par][:, p, :, :], bank[:, None, p * D:(p + 1) * D].to_broadcast([P, NK - 1, D]),
                                          statepow[:], ALU.mult)
                i.then_inc(dve_taken, 1)

            def norm_stats(src, h, st, mv_, ve_, done, before):
                for i in range(2):
                    dve.bn_stats(st[:, 2 * h + i, :], src[i]).then_inc(done, 1)
                dve.wait_ge(done, before + 2)
                dve.memset(waited[:], 0.0)
                for i in range(2):
                    dve.bn_aggr(mv_[:, 2 * h + i, :], st[:, 2 * h + i, :]).then_inc(done, 1)
                dve.wait_ge(done, before + 4)
                dve.tensor_scalar(ve_[:, 2 * h:2 * h + 2], mv_[:, 2 * h:2 * h + 2, 1], EPS, None, ALU.add).then_inc(done, 1)

            def first_norm(s):
                m = s.n - 1
                dve.wait_ge(rstd_ready, 2 * m)
                dve.wait_ge(yb_ready, 2 * m)
                dve.wait_ge(act_filled, s.a0)
                for h in range(2):
                    dve.wait_ge(dve_filled, s.dve("out", h) + 1)
                    bank = v_bank(s, "out", h)
                    src = [bank[:, i * E:(i + 1) * E] for i in range(2)]
                    norm_stats(src, h, stats, mv, ve, stats_done, 10 * m + 5 * h)
                    for i in range(2):
                        q = dve.scalar_tensor_tensor(y[:, 2 * h + i, :], src[i], mv[:, 2 * h + i, 0:1], gam0[:],
                                                     ALU.subtract, ALU.mult)
                    q.then_inc(dve_taken, 1)

            def first_residual(s):
                m = s.n - 1
                dve.wait_ge(dve_taken, s.dve("out", 1) + 1)
                dve.wait_ge(xbeta_ready, s.n)
                for p in range(PAIRS):
                    if p % 2 == 0:
                        dve.wait_ge(rstd_ready, 2 * m + 1 + p // 2)
                    dve.scalar_tensor_tensor(y[:, p, :], y[:, p, :], rstd[:, p:p + 1], xn[:, p, :],
                                             ALU.mult, ALU.add).then_inc(y_ready, 1)

            def second_norm(s):
                m = s.n - 1
                r = rows[1 - s.par]
                dve.wait_ge(yb_ready, 2 * s.n)
                dve.wait_ge(stored, 16 * m)
                dve.wait_ge(rstd2_ready, 2 * m)
                for h in range(2):
                    two = slice(2 * h, 2 * h + 2)
                    dve.wait_ge(dve_filled, s.dve("w2", h) + 1)
                    dve.tensor_tensor(z[:, two, :], v_bank(s, "w2", h)[:].rearrange("t (i c) -> t i c", i=2), r[:, two, 0, :],
                                      ALU.add).then_inc(dve_taken, 1)
                    dve.wait_ge(dve_taken, s.dve("w2", h) + 1)
                    norm_stats([z[:, 2 * h + i, :] for i in range(2)], h, stats2, mv2, ve2, stats2_done, 14 * m + 7 * h)
                    for i in range(2):
                        p = 2 * h + i
                        q = dve.scalar_tensor_tensor(z[:, p, :], z[:, p, :], mv2[:, p, 0:1], r[:, p, 1, :],
                                                     ALU.subtract, ALU.mult)
                        q.then_inc(stats2_done, 1)

            def second_residual(s):
                m = s.n - 1
                for p in range(PAIRS):
                    dve.wait_ge(stats2_done, 14 * m + 7 * (p // 2) + 6 + p % 2)
                    if p % 2 == 0:
                        dve.wait_ge(rstd2_ready, 2 * m + 1 + p // 2)
                    dve.scalar_tensor_tensor(z[:, p, :], z[:, p, :], rstd2[:, p:p + 1], rows[1 - s.par][:, p, 2, :],
                                             ALU.mult, ALU.add).then_inc(out_ready, 1)

            def blended_states(s, k):
                if k > 2:
                    dve.wait_ge(act_filled, s.act("carry", k - 2) + 1)
                elif s is not FIRST:
                    dve.wait_ge(act_filled, s.a0)
                for p in range(PAIRS):
                    dve.wait_ge(dve_filled, s.dve(f"state{k}", p) + 1)
                    dve.tensor_tensor(state[:, k % 2, p, :].rearrange("d (b c) -> d b c", b=2),
                                      v_bank(s, f"state{k}", p)[:].rearrange("d (b c) -> d b c", b=2),
                                      bw[:, None, :].to_broadcast([P, 2, E]), ALU.mult).then_inc(dve_taken, 1)

            def add_carried(s):
                dve.wait_ge(lags_added, LAG_ADDS * (s.n + 1))
                for k in range(1, NK):
                    dve.wait_ge(dve_filled, s.dve("carryT", k) + 1)
                    to = temporal[s.par][:].rearrange("c e b (p k) -> c e (b p) k", k=NK)[:, :, :, k]
                    dve.tensor_tensor(to, to, v_bank(s, "carryT", k)[:, 0:EH * P].rearrange("c (e r) -> c e r", e=EH),
                                      ALU.add).then_inc(dve_taken, 1)

            def one_pass(s):
                if s.front:
                    context(s)
                if s.heavy:
                    lag_products(s, 0, 0, 4)
                if s.tail:
                    gated_soma(s)
                if s.heavy:
                    lag_products(s, 0, 4, 6)
                if s.tail:
                    first_norm(s)
                if s.heavy:
                    lag_products(s, 0, 6, 8)
                if s.tail:
                    first_residual(s)
                if s.heavy:
                    lag_products(s, 0, 8, LAGS)
                    lag_products(s, 1, 0, 1)
                if s.front:
                    gated_x(s)
                if s.heavy:
                    lag_products(s, 1, 1, 4)
                if s.front:
                    front_mod(s)
                if s.heavy:
                    lag_products(s, 1, 4, 6)
                if s.front:
                    decayed_mod(s)
                if s.heavy:
                    lag_products(s, 1, 6, LAGS)
                if s.tail:
                    second_norm(s)
                if s.heavy:
                    blended_states(s, 1)
                if s.tail:
                    second_residual(s)
                if s.heavy:
                    blended_states(s, 2)
                    blended_states(s, 3)
                    add_carried(s)

            count = [0]

            def step(instruction):
                count[0] += 1
                instruction.then_inc(dve_const, 1)
                dve.wait_ge(dve_const, count[0])

            dve.wait_ge(act_const, 2)
            dve.wait_ge(pool_const, 3)
            a = alpha[:, 0:1]
            step(dve.tensor_copy(powsq[:, 0:1], a))
            for i in range(1, 6):
                step(dve.tensor_tensor(powsq[:, i:i + 1], powsq[:, i - 1:i], powsq[:, i - 1:i], ALU.mult))
            step(dve.memset(revpow[:, T - 1:T], 1.0))
            for i in range(6):
                m = 1 << i
                step(dve.tensor_scalar(revpow[:, T - 2 * m:T - m], revpow[:, T - m:T], powsq[:, i:i + 1], None, ALU.mult))
            step(dve.memset(carrypow[:], 0.0))
            step(dve.tensor_copy(carrypow[:, L:L + 1], a))
            for i in range(4):
                m = 1 << i
                step(dve.tensor_scalar(carrypow[:, L + m:L + 2 * m], carrypow[:, L:L + m], powsq[:, i:i + 1], None, ALU.mult))
            step(dve.memset(statepow_t, 0.0))
            for k in range(1, NK):
                for b in range(2):
                    row = statepow_t[:, k - 1, b * T:(b + 1) * T].rearrange("d (p q) -> d q p", q=NK)
                    step(dve.tensor_copy(row[:, 0:k, :], revpow[:, T - k * L:T].rearrange("d (q p) -> d q p", p=L)))
            step(dve.memset(decay[:], 1.0))
            step(dve.tensor_scalar(decay[:], decay[:], alpha[:, 1:2], None, ALU.mult))
            step(dve.memset(decay[:].rearrange("c (b t) -> c b t", t=T)[:, :, 0:1], 0.0))
            step(dve.tensor_copy(lang[:], lang_i[:]))
            step(dve.tensor_copy(idf[:], ids_l[:]))
            step(dve.tensor_scalar(onehot[:], idf[:], lang[:], None, ALU.is_equal))
            assert count[0] == DVE_TABLES, count
            dve.wait_ge(pe_const, 2)
            step(dve.tensor_reduce(smax[:], abank[0][:, 0:EH * P].rearrange("c (e d) -> c e d", e=EH), AX.X, ALU.max))
            step(dve.tensor_scalar(smax[:], smax[:], -1.0, None, ALU.mult))
            assert count[0] == DVE_MAX, count
            dve.wait_ge(act_const, ACT_ALL)
            step(dve.reciprocal(srec[:], ssum[:]))
            for e in range(EH):
                step(dve.tensor_scalar(soma[0][:, e, 0:P], soma[1][:, e, 0:P], srec[:, e:e + 1], None, ALU.mult))
            assert count[0] == DVE_SOFTMAX, count
            dve.wait_ge(pe_const, PE_ALL)
            step(dve.tensor_copy(bw, abank[3][:, 0:E]))
            for j in range(1, L):
                step(dve.tensor_scalar(lagw[:, j, :], lagw[:, j - 1, :], a, None, ALU.mult))
            assert count[0] == DVE_ALL, count
            one_pass(FILL)
            one_pass(FIRST)
            one_pass(SECOND)
            with dve.Fori(0, LOOPS) as j:
                for u in range(2):
                    one_pass(loop_pass(j, u))
            one_pass(SECOND_LAST)
            one_pass(LAST)
            one_pass(DRAIN)


def kernel(x, condB_tauraws, cond_256, condB_bn2, cond_1024, itok_B_0_8, L0_cond_tau_ctx, L0_cond_Wg, L0_cond_bg,
           L0_cond_Wn1, L0_cond_bn1, L0_cond_Wsoma, L0_cond_bsoma, L0_cond_Wtemp, L0_cond_btemp, L0_cond_Wout,
           L0_cond_gamma, L0_cond_beta, L1_cond_W1, L1_cond_b1, L1_cond_W2, L1_cond_b2, L1_cond_gamma, L1_cond_beta):
    import numpy as np
    import concourse.bacc as bacc
    from concourse.bass_utils import run_bass_kernel_spmd

    def turned(a):
        return np.ascontiguousarray(np.asarray(a).T)

    rows = np.asarray(x).reshape(B * T, E)
    inputs = [
        ("xT", turned(rows)), ("x", rows), ("tau", condB_tauraws), ("wn2T", turned(cond_256)), ("bn2", condB_bn2),
        ("blend", cond_1024), ("ids", np.asarray(itok_B_0_8).reshape(1, B)),
        ("tauc", np.asarray(L0_cond_tau_ctx).reshape(1, 1)), ("wgT", turned(L0_cond_Wg)), ("bg", L0_cond_bg),
        ("wn1T", turned(L0_cond_Wn1)), ("bn1", L0_cond_bn1), ("wsT", turned(L0_cond_Wsoma)), ("bs", L0_cond_bsoma),
        ("wtT", turned(L0_cond_Wtemp)), ("bt", L0_cond_btemp), ("woT", turned(L0_cond_Wout)),
        ("gamma", L0_cond_gamma), ("beta", L0_cond_beta), ("w1", L1_cond_W1), ("b1", L1_cond_b1), ("w2", L1_cond_W2),
        ("rows", np.concatenate([np.asarray(a) for a in (L1_cond_b2, L1_cond_gamma, L1_cond_beta)], axis=1)),
    ]
    nc = bacc.Bacc("TRN2", target_bir_lowering=False, num_devices=1)
    arrays, args = {}, []
    for name, a in inputs:
        a = np.ascontiguousarray(a)
        arrays[f"in_{name}"] = a
        args.append(nc.dram_tensor(f"in_{name}", a.shape, mybir.dt.from_np(a.dtype), kind="ExternalInput").ap())
    out = nc.dram_tensor("out_dram", (B * T, E), F32, kind="ExternalOutput").ap()
    build(nc, *args, out)
    r = run_bass_kernel_spmd(nc, [arrays], core_ids=[0])
    return r.results[0]["out_dram"].reshape(B, T, E)
```

```python
from contextlib import ExitStack

import concourse.bass as bass
from concourse import mybir

F32 = mybir.dt.float32
F32R = mybir.dt.float32r
I32 = mybir.dt.int32
ALU = mybir.AluOpType
ACT = mybir.ActivationFunctionType
AX = mybir.AxisListType

P = 128
B, T, E, D = 128, 64, 256, 128
H = 64
L = 16
NK = T // L
SEQ = 8
TOK = SEQ * T
TILES = B // SEQ
PAIRS = SEQ // 2
EH = E // P
LAGS = L // 2 + 1
EPS = 1e-5
RING = 4


class Pass:

    def __init__(self, n, par, half, act_before, dve_before, phases=None, heavy=True, tail=True, front=True):
        self.n, self.par, self.heavy, self.tail, self.front = n, par, heavy, tail, front
        self.tail_loads = half + par
        a, v = [], []
        if tail:
            a += [("temp", e) for e in range(EH)]
        if front:
            a += [("n1", 0), ("soma", 0)]
        if front:
            a += [("wg", 0)]
        if tail:
            a += [("yT", e) for e in range(EH)]
        if tail:
            a += [("w1", 0)]
        if front:
            a += [("n2", 0), ("wg", 1), ("soma", 1)] + [("gnat", s) for s in range(2)]
        if heavy:
            a += [("carry", k) for k in range(1, NK)]
            v += [("lag0", j) for j in range(5)]
        if tail:
            v += [("out", s) for s in range(2)]
        if heavy:
            v += [("lag0", j) for j in range(5, LAGS)] + [("lag1", j) for j in range(4)]
        if tail:
            v += [("w2", 0)]
        if heavy:
            v += [("lag1", j) for j in range(4, 6)]
        if tail:
            v += [("w2", 1)]
        if heavy:
            v += [("lag1", j) for j in range(6, LAGS)]
            v += [(f"state{k}", p) for k in range(1, 3) for p in range(PAIRS)]
        if front:
            v += [("modnat", 0)]
        if heavy:
            v += [("state3", p) for p in range(PAIRS)]
            v += [("carryT", k) for k in range(1, NK)]
        self.a_order, self.v_order = a, v
        self.a0, self.v0 = act_before, dve_before
        self.phases = phases or (act_before % RING, dve_before % RING)

    def act(self, name, k=0):
        return self.a0 + self.a_order.index((name, k))

    def dve(self, name, k=0):
        return self.v0 + self.v_order.index((name, k))

    def act_bank(self, banks, name, k=0):
        return banks[(self.phases[0] + self.a_order.index((name, k))) % RING]

    def dve_bank(self, banks, name, k=0):
        return banks[(self.phases[1] + self.v_order.index((name, k))) % RING]

    def next_act(self):
        return self.a0 + len(self.a_order)

    def next_dve(self):
        return self.v0 + len(self.v_order)


FILL = Pass(-1, 1, -1, 0, 0, heavy=False, tail=False)
FIRST = Pass(0, 0, 0, FILL.next_act(), FILL.next_dve(), tail=False)
SECOND = FULL = Pass(1, 1, 0, FIRST.next_act(), FIRST.next_dve())
FULL_ACT, FULL_DVE = len(FULL.a_order), len(FULL.v_order)
assert 2 * FULL_ACT % RING == 0 and 2 * FULL_DVE % RING == 0


def loop_pass(j, u):
    a, v = SECOND.next_act() + FULL_ACT * u, SECOND.next_dve() + FULL_DVE * u
    return Pass(2 * j + u + 2, u, j + 1, 2 * FULL_ACT * j + a, 2 * FULL_DVE * j + v, (a % RING, v % RING))


LOOPS = (TILES - 4) // 2
SECOND_LAST = Pass(TILES - 2, 0, TILES // 2 - 1, FULL.a0 + FULL_ACT * (TILES - 3), FULL.v0 + FULL_DVE * (TILES - 3))
LAST = Pass(TILES - 1, 1, TILES // 2 - 1, SECOND_LAST.next_act(), SECOND_LAST.next_dve(), front=False)
DRAIN = Pass(TILES, 0, TILES // 2, LAST.next_act(), LAST.next_dve(), heavy=False, front=False)

POOL_ALL = 7
POOL_SPLIT = POOL_ALL + 3 + 2
PE_TURNS, PE_ALL = EH + NK, EH + NK + EH
ACT_HIGH = 2 + 3
ACT_ALL = ACT_HIGH + (NK - 1) + 1 + EH
ACT_SPLIT = ACT_ALL + 2
DVE_TABLES, DVE_MAX, DVE_SOFTMAX, DVE_ALL = 32, 34, 37, 53


def prod_slot(e, j):
    return (e * (LAGS - 1) + j - 1) % PRODS


PRODS = 4


def build(nc, xT_d, x_d, tau_d, wn2T_d, bn2_d, blend_d, ids_d, tauc_d, wgT_d, bg_d, wn1T_d, bn1_d,
          wsT_d, bs_d, wtT_d, bt_d, woT_d, gamma_d, beta_d, w1_d, b1_d, w2_d, rows_d, out_d):
    NL = w1_d.shape[0]
    ctx = ExitStack()
    with ctx:
        def sb(name, shape, dt=F32):
            return ctx.enter_context(nc.sbuf_tensor(name, shape, dt))

        def sem(name):
            return ctx.enter_context(nc.semaphore(name))

        ident = sb("ident", [P, P])
        wgx = sb("wgx", [P, 2, EH, E], F32R)
        wn1 = sb("wn1", [P, 2, EH, H], F32R)
        ws = sb("ws", [P, 2, EH, E], F32R)
        wgc = sb("wgc", [P, EH, E])
        wn2 = sb("wn2", [H, D])
        wt = sb("wt", [P, EH, E])
        wo = sb("wo", [P, EH, E])
        cols = sb("cols", [P, 10])
        bgc, bsc, btc = (cols[:, 2 * i:2 * i + 2] for i in range(3))
        bn1c, bn2c = cols[0:H, 6:7], cols[:, 7:8]
        tauc = cols[:, 8:9]
        taud = cols[:, 9:10]
        alpha = sb("alpha", [P, 2])
        gam0 = sb("gam0", [P, E])
        bet0 = sb("bet0", [P, E])
        bw = sb("bw", [P, E])[:]
        lagw = sb("lagw", [P, 2, LAGS, E], F32R)
        lagw_far = sb("lagw_far", [P, L - LAGS, E])
        revpow = sb("revpow", [P, T])
        powsq = sb("powsq", [P, 8])
        carrypow = sb("carrypow", [P, 3 * L])
        statepow = sb("statepow", [P, NK - 1, D])
        decay = sb("decay", [P, TOK])
        ids = sb("ids", [1, B], I32)
        ids_l = sb("ids_l", [NL, B], I32)
        lang_i = sb("lang_i", [NL, 1], I32)
        lang = sb("lang", [NL, 1])
        idf = sb("idf", [NL, B])
        onehot = sb("onehot", [NL, B])
        b1d = sb("b1d", [NL, 2 * H])
        b1g = sb("b1g", [P, B])
        smax = sb("smax", [P, EH])
        ssum = sb("ssum", [P, EH])
        srec = sb("srec", [P, EH])
        waited = sb("waited", [1, 1])
        minus_half = sb("minus_half", [P, PAIRS])

        xT = sb("xT", [P, EH, TOK])
        xs = sb("xs", [P, 2, EH, TOK], F32R)
        xn = sb("xn", [P, PAIRS, E])
        rows = sb("rows", [P, PAIRS, 3, E])
        w1 = sb("w1", [P, PAIRS, EH, 2 * H])
        w2 = sb("w2", [P, PAIRS, E])
        ctxT = sb("ctxT", [P, EH, TOK])
        h1 = sb("h1", [H, TOK])
        soma = [sb(f"soma{i}", [P, EH, TOK]) for i in range(2)]
        g = [sb(f"g{i}", [P, EH, SEQ, T]) for i in range(2)]
        mod = [sb(f"mod{i}", [P, SEQ, T]) for i in range(2)]
        mods = [sb(f"mods{i}", [P, 2, SEQ, T], F32R) for i in range(2)]
        temporal = [sb(f"temporal{i}", [P, EH, SEQ, T]) for i in range(2)]
        gnat = [sb(f"gnat{i}", [P, PAIRS, 2, E]) for i in range(2)]
        decmod = [sb(f"decmod{i}", [P, PAIRS, NK - 1, D]) for i in range(2)]
        prod = sb("prod", [P, PRODS, TOK])
        statepow_t = prod[:, 0, 0:(NK - 1) * P].rearrange("d (k t) -> d k t", t=P)
        lagw_raw = prod[:].rearrange("d s t -> d (s t)").rearrange("d (j c) -> d j c", c=E)
        state = sb("state", [P, 2, PAIRS, 2 * E])
        raw = state[:].rearrange("c a p e -> c (a p e)")
        wgx_raw = raw[:, 0:EH * E].rearrange("c (k e) -> c k e", e=E)
        ws_raw = raw[:, EH * E:2 * EH * E].rearrange("c (k e) -> c k e", e=E)
        wn1_raw = raw[:, 2 * EH * E:2 * EH * E + EH * H].rearrange("c (k e) -> c k e", e=H)
        carry = sb("carry", [P, NK, E])
        gate = sb("gate", [P, EH, TOK])
        y = sb("y", [P, PAIRS, E])
        z = y
        gs = gate
        yT = gs
        hid = sb("hid", [P, PAIRS, P])
        stats = sb("stats", [P, PAIRS, 6])
        mv = sb("mv", [P, PAIRS, 2])
        ve = sb("ve", [P, PAIRS])
        rstd = sb("rstd", [P, PAIRS])
        stats2 = sb("stats2", [P, PAIRS, 6])
        mv2 = sb("mv2", [P, PAIRS, 2])
        ve2 = sb("ve2", [P, PAIRS])
        rstd2 = sb("rstd2", [P, PAIRS])

        abank = [ctx.enter_context(nc.psum_tensor(f"abank{i}", [P, 512], F32)) for i in range(RING)]
        vbank = [ctx.enter_context(nc.psum_tensor(f"vbank{i}", [P, 512], F32)) for i in range(RING)]

        act_filled = sem("act_filled")
        act_taken = sem("act_taken")
        dve_filled = sem("dve_filled")
        dve_taken = sem("dve_taken")
        const_loaded = sem("const_loaded")
        ids_loaded = sem("ids_loaded")
        pool_const = sem("pool_const")
        dve_const = sem("dve_const")
        act_const = sem("act_const")
        pe_const = sem("pe_const")
        xT_loaded = sem("xT_loaded")
        xn_loaded = sem("xn_loaded")
        rows_loaded = sem("rows_loaded")
        w1_loaded = sem("w1_loaded")
        w2_loaded = sem("w2_loaded")
        xs_high = sem("xs_high")
        xs_low = sem("xs_low")
        mods_high = sem("mods_high")
        mods_low = sem("mods_low")
        ctx_ready = sem("ctx_ready")
        g_ready = sem("g_ready")
        gs_ready = sem("gs_ready")
        mod_ready = sem("mod_ready")
        lags_added = sem("lags_added")
        xbeta_ready = sem("xbeta_ready")
        stats_done = sem("stats_done")
        rstd_ready = sem("rstd_ready")
        y_ready = sem("y_ready")
        yb_ready = sem("yb_ready")
        stats2_done = sem("stats2_done")
        rstd2_ready = sem("rstd2_ready")
        out_ready = sem("out_ready")
        stored = sem("stored")

        LAG_ADDS = 2 * (2 * (LAGS - 2) + 1)

        def by_chunk_step(ap):
            return ap.rearrange("c (b p k) -> c b k p", b=SEQ, k=NK)

        def in_time(ap):
            return ap.rearrange("c (b k p) -> c b k p", b=SEQ, k=NK)

        def flat(buf):
            return buf[:].rearrange("d b t -> d (b t)")

        def pair_rows(dram, n):
            return dram[bass.ds(n * TOK, TOK), :].rearrange("(p t) c -> t p c", p=PAIRS)

        block = ctx.enter_context(nc.Block())

        CONST_LOADS = 23

        @block.sync
        def _(sp):
            def load_xT(n):
                sp.dma_start(xT[:], xT_d[:, bass.ds(n * TOK, TOK)].rearrange("(k p) t -> p k t", p=P))\
                    .then_inc(xT_loaded, 16)

            def load_adapters(n):
                for q in range(SEQ):
                    lang_q = sp.value_load(ids[0:1, bass.ds(n * SEQ + q, 1)], min_val=0, max_val=NL - 1)
                    half = slice((q % 2) * T, (q % 2 + 1) * T)
                    sp.dma_start(w1[:, q // 2, :, (q % 2) * H:(q % 2 + 1) * H], w1_d[bass.ds(lang_q, 1), :, :].rearrange("l (k c) a -> c (l k) a", k=EH))\
                        .then_inc(w1_loaded, 16)
                    sp.dma_start(w2[half, q // 2, :], w2_d[bass.ds(lang_q, 1), :, :].rearrange("l a c -> (l a) c"))\
                        .then_inc(w2_loaded, 16)
                    sp.dma_start(rows[half, q // 2, :, :].rearrange("t r c -> t (r c)"),
                                 rows_d[bass.ds(lang_q, 1), :].to_broadcast([T, 3 * E]))\
                        .then_inc(rows_loaded, 16)

            sp.dma_start(ids[:], ids_d).then_inc(ids_loaded, 16)
            sp.dma_start(taud, tau_d.rearrange("(d a) -> d a", a=1)).then_inc(const_loaded, 16)
            sp.dma_start(tauc, tauc_d.to_broadcast([P, 1])).then_inc(const_loaded, 16)
            load_xT(0)
            for w, src in ((wgx_raw, wgT_d[0:E, :]), (ws_raw, wsT_d), (wn1_raw, wn1T_d), (wgc, wgT_d[E:2 * E, :]), (wt, wtT_d), (wo, woT_d)):
                sp.dma_start(w[:] if w in (wgc, wt, wo) else w, src.rearrange("(k c) e -> c k e", c=P)).then_inc(const_loaded, 16)
            sp.dma_start(wn2[:], wn2T_d).then_inc(const_loaded, 16)
            sp.dma_start(bw, blend_d).then_inc(const_loaded, 16)
            for c, src in ((bgc, bg_d), (bsc, bs_d), (btc, bt_d)):
                for e in range(EH):
                    sp.dma_start(c[:, e:e + 1], src[e * P:(e + 1) * P].rearrange("(p a) -> p a", a=1))\
                        .then_inc(const_loaded, 16)
            sp.dma_start(bn1c, bn1_d.rearrange("(p a) -> p a", a=1)).then_inc(const_loaded, 16)
            sp.dma_start(bn2c, bn2_d.rearrange("(p a) -> p a", a=1)).then_inc(const_loaded, 16)
            sp.dma_start(gam0[:], gamma_d.rearrange("(a c) -> a c", a=1).to_broadcast([P, E])).then_inc(const_loaded, 16)
            sp.dma_start(bet0[:], beta_d.rearrange("(a c) -> a c", a=1).to_broadcast([P, E])).then_inc(const_loaded, 16)
            sp.dma_start(ids_l[:], ids_d.to_broadcast([NL, B])).then_inc(const_loaded, 16)
            for h in range(2):
                sp.dma_start(b1d[:, h * H:(h + 1) * H], b1_d).then_inc(const_loaded, 16)
            sp.wait_ge(ids_loaded, 16)

            def one_pass(s):
                n = s.n
                if s.tail:
                    sp.wait_ge(y_ready, PAIRS * n)
                if s.heavy:
                    sp.dma_start(xn[:], pair_rows(x_d, n)).then_inc(xn_loaded, 16)
                if s.front and s is not SECOND_LAST:
                    sp.wait_ge(g_ready, EH * (n + 2))
                    load_xT(n + 2)
                if s.tail:
                    sp.wait_ge(out_ready, PAIRS * n)
                    sp.dma_start(pair_rows(out_d, n - 1), z[:]).then_inc(stored, 16)
                if s.heavy:
                    load_adapters(n)

            one_pass(FILL)
            one_pass(FIRST)
            one_pass(SECOND)
            with sp.Fori(0, LOOPS) as j:
                for u in range(2):
                    one_pass(loop_pass(j, u))
            one_pass(SECOND_LAST)
            one_pass(LAST)
            one_pass(DRAIN)
            sp.wait_ge(stored, 16 * TILES)

        @block.tensor
        def _(pe):
            def fill_act(use):
                if not isinstance(use, int) or use >= RING:
                    pe.wait_ge(act_taken, use - (RING - 1))

            def fill_dve(use):
                if not isinstance(use, int) or use >= RING:
                    pe.wait_ge(dve_taken, use - (RING - 1))

            def a_bank(s, name, k=0):
                return s.act_bank(abank, name, k)

            def v_bank(s, name, k=0):
                return s.dve_bank(vbank, name, k)

            def dense(bank, w, srcs, e, stop=True):
                for i, (k, src) in enumerate(srcs):
                    last = pe.matmul(bank[:], w[:, k, e * P:(e + 1) * P], src,
                                     start=(i == 0), stop=stop and i == len(srcs) - 1)
                return last

            def split_matmul(out, w, x, start=True, stop=True):
                for i, (a, b) in enumerate(((0, 1), (1, 0), (0, 0))):
                    last = pe.matmul(out, w(a), x(b), start=start and i == 0, stop=stop and i == 2)
                return last

            def split_dense(bank, w, e, width=P, m=P, start=True):
                for k in range(EH):
                    last = split_matmul(bank[0:m, :], lambda a: w[:, a, k, e * P:e * P + width], lambda a: xs[:, a, k, :],
                                        start and k == 0, k == EH - 1)
                return last

            def lag_bank(s, e, j):
                name = f"lag{e}"
                fill_dve(s.dve(name, j))
                bank = v_bank(s, name, j)[:].rearrange("c (b t) -> c b t", b=SEQ)
                m = mod[s.par]
                last = split_matmul(bank[:, :, NK * j:T], lambda a: lagw[:, a, j, e * P:(e + 1) * P],
                                    lambda a: mods[s.par][:, a, :, 0:NK * (L - j)])
                if 0 < j < L // 2:
                    last = pe.matmul(bank[:, :, 0:NK * j], lagw_far[:, L - j - LAGS, e * P:(e + 1) * P], m[:, :, 0:NK * j],
                                     start=True, stop=True)
                last.then_inc(dve_filled, 1)

            def front_gate(s, e):
                fill_act(s.act("wg", e))
                pe.wait_ge(ctx_ready, 2 * s.n + 4)
                dense(a_bank(s, "wg", e), wgc, [(k, ctxT[:, k, :]) for k in range(EH)], e, stop=False)
                split_dense(a_bank(s, "wg", e), wgx, e, start=False).then_inc(act_filled, 1)

            def front_n1(s):
                pe.wait_ge(xs_high, s.n + 2)
                pe.wait_ge(xs_low, s.n + 2)
                fill_act(s.act("n1"))
                split_dense(a_bank(s, "n1"), wn1, 0, H, H).then_inc(act_filled, 1)

            def front_soma(s, e):
                fill_act(s.act("soma", e))
                split_dense(a_bank(s, "soma", e), ws, e).then_inc(act_filled, 1)

            def front_mod(s):
                pe.wait_ge(act_taken, s.act("n1") + 1)
                fill_act(s.act("n2"))
                pe.matmul(a_bank(s, "n2")[:], wn2[:], h1[:], start=True, stop=True).then_inc(act_filled, 1)

            def g_by_token(s):
                f = s.n + 1
                pe.wait_ge(g_ready, EH * (f + 1))
                for h in range(2):
                    fill_act(s.act("gnat", h))
                    for i in range(2):
                        p = 2 * h + i
                        for e in range(EH):
                            last = pe.transpose(a_bank(s, "gnat", h)[:, i * E + e * P:i * E + (e + 1) * P],
                                                g[1 - s.par][:, e, 2 * p:2 * p + 2, :].rearrange("c b t -> c (b t)"), ident[:])
                    last.then_inc(act_filled, 1)

            def mod_by_token(s):
                pe.wait_ge(mod_ready, s.n + 2)
                fill_dve(s.dve("modnat"))
                for p in range(PAIRS):
                    last = pe.transpose(v_bank(s, "modnat")[:, p * D:(p + 1) * D],
                                        mod[1 - s.par][:, 2 * p:2 * p + 2, :].rearrange("d b t -> d (b t)"), ident[:])
                last.then_inc(dve_filled, 1)

            def tail_temporal(s):
                pe.wait_ge(dve_taken, s.v0)
                for e in range(EH):
                    fill_act(s.act("temp", e))
                    src = temporal[1 - s.par]
                    dense(a_bank(s, "temp", e), wt, [(k, src[:, k, :, :].rearrange("c b t -> c (b t)")) for k in range(EH)], e)\
                        .then_inc(act_filled, 1)

            def tail_out(s):
                pe.wait_ge(gs_ready, EH * s.n)
                for h in range(2):
                    fill_dve(s.dve("out", h))
                    for i in range(2):
                        p = 2 * h + i
                        for k in range(EH):
                            last = pe.matmul(v_bank(s, "out", h)[:, i * E:(i + 1) * E], gs[:, k, p * P:(p + 1) * P],
                                             wo[:, k, :], start=(k == 0), stop=(k == EH - 1))
                    last.then_inc(dve_filled, 1)

            def tail_yT(s):
                pe.wait_ge(y_ready, PAIRS * s.n)
                for e in range(EH):
                    fill_act(s.act("yT", e))
                    for p in range(PAIRS):
                        last = pe.transpose(a_bank(s, "yT", e)[:, p * P:(p + 1) * P], y[:, p, e * P:(e + 1) * P], ident[:])
                    last.then_inc(act_filled, 1)

            def tail_w1(s):
                pe.wait_ge(act_taken, s.act("yT", 1) + 1)
                pe.wait_ge(w1_loaded, 16 * SEQ * s.n)
                fill_act(s.act("w1"))
                for p in range(PAIRS):
                    for k in range(EH):
                        last = pe.matmul(a_bank(s, "w1")[:, p * P:(p + 1) * P], w1[:, p, k, :],
                                         yT[:, k, p * P:(p + 1) * P], start=(k == 0), stop=(k == EH - 1))
                last.then_inc(act_filled, 1)

            def tail_w2(s, h):
                if h == 0:
                    pe.wait_ge(act_taken, s.act("w1") + 1)
                    pe.wait_ge(w2_loaded, 16 * SEQ * s.n)
                fill_dve(s.dve("w2", h))
                for i in range(2):
                    p = 2 * h + i
                    last = pe.matmul(v_bank(s, "w2", h)[:, i * E:(i + 1) * E], hid[:, p, :], w2[:, p, :],
                                     start=True, stop=True)
                last.then_inc(dve_filled, 1)

            def states(s, k):
                for p in range(PAIRS):
                    fill_dve(s.dve(f"state{k}", p))
                    pe.matmul(v_bank(s, f"state{k}", p)[:], decmod[s.par][:, p, k - 1, :],
                              gnat[s.par][:, p, :, :].rearrange("t b c -> t (b c)"), start=True, stop=True)\
                        .then_inc(dve_filled, 1)

            def carried(s, k):
                fill_act(s.act("carry", k))
                pe.wait_ge(dve_taken, s.dve(f"state{k}", PAIRS - 1) + 1)
                bank = a_bank(s, "carry", k)
                for b in range(2):
                    for p in range(PAIRS):
                        last = pe.matmul(bank[2 * L * p:2 * L * (p + 1), 0:E], carrypow[:, L * (1 - b):L * (3 - b)],
                                         state[:, k % 2, p, b * E:(b + 1) * E], start=(b == 0), stop=(b == 1))
                last.then_inc(act_filled, 1)

            def carried_T(s, k):
                pe.wait_ge(act_taken, s.act("carry", k) + 1)
                fill_dve(s.dve("carryT", k))
                for e in range(EH):
                    last = pe.transpose(v_bank(s, "carryT", k)[:, e * P:(e + 1) * P], carry[:, k, e * P:(e + 1) * P], ident[:])
                last.then_inc(dve_filled, 1)

            def one_pass(s):
                def lags(e, j0, j1):
                    if s.heavy:
                        for j in range(j0, j1):
                            lag_bank(s, e, j)
                if s.heavy:
                    pe.wait_ge(mod_ready, s.n + 1)
                    pe.wait_ge(mods_high, s.n + 1)
                    pe.wait_ge(mods_low, s.n + 1)
                lags(0, 0, 3)
                if s.tail:
                    tail_temporal(s)
                lags(0, 3, 5)
                if s.tail:
                    tail_out(s)
                if s.front:
                    front_n1(s)
                    front_soma(s, 0)
                lags(0, 5, LAGS)
                if s.front:
                    front_gate(s, 0)
                lags(1, 0, 1)
                if s.tail:
                    tail_yT(s)
                lags(1, 1, 2)
                if s.tail:
                    tail_w1(s)
                if s.front:
                    front_mod(s)
                lags(1, 2, 4)
                if s.tail:
                    tail_w2(s, 0)
                if s.front:
                    front_gate(s, 1)
                lags(1, 4, 6)
                if s.tail:
                    tail_w2(s, 1)
                if s.front:
                    front_soma(s, 1)
                lags(1, 6, LAGS)
                if s.heavy:
                    states(s, 1)
                if s.front:
                    g_by_token(s)
                if s.heavy:
                    states(s, 2)
                if s.front:
                    mod_by_token(s)
                if s.heavy:
                    carried(s, 1)
                    states(s, 3)
                    carried(s, 2)
                    carried(s, 3)
                    for k in range(1, NK):
                        carried_T(s, k)

            pe.wait_ge(pool_const, 2)
            pe.wait_ge(const_loaded, 16 * CONST_LOADS)
            for e in range(EH):
                pe.transpose(abank[0][:, e * P:(e + 1) * P], bw[:, e * P:(e + 1) * P], ident[:]).then_inc(pe_const, 1)
            pe.wait_ge(dve_const, DVE_TABLES)
            for k in range(1, NK):
                pe.transpose(abank[1][:, (k - 1) * P:k * P], statepow_t[:, k - 1, :], ident[:]).then_inc(pe_const, 1)
            pe.matmul(abank[2][:, 0:B], b1d[:], onehot[:], start=True, stop=True).then_inc(pe_const, 1)
            pe.wait_ge(dve_const, DVE_SOFTMAX)
            for e in range(EH):
                pe.transpose(abank[3][:, e * P:(e + 1) * P], soma[0][:, e, 0:P], ident[:]).then_inc(pe_const, 1)
            pe.wait_ge(dve_const, DVE_ALL)
            pe.wait_ge(act_const, ACT_SPLIT)
            pe.wait_ge(pool_const, POOL_SPLIT)
            one_pass(FILL)
            one_pass(FIRST)
            one_pass(SECOND)
            with pe.Fori(0, LOOPS) as j:
                for u in range(2):
                    one_pass(loop_pass(j, u))
            one_pass(SECOND_LAST)
            one_pass(LAST)
            one_pass(DRAIN)

        @block.scalar
        def _(act):
            def a_bank(s, name, k=0):
                return s.act_bank(abank, name, k)

            def temporal_gate(s):
                for e in range(EH):
                    act.wait_ge(act_filled, s.act("temp", e) + 1)
                    act.activation(in_time(gate[:, e, :]), by_chunk_step(a_bank(s, "temp", e)[:]),
                                   ACT.Sigmoid, bias=btc[:, e:e + 1]).then_inc(act_taken, 1)

            def front_hidden(s):
                act.wait_ge(act_filled, s.act("n1") + 1)
                act.activation(h1[:], a_bank(s, "n1")[0:H, :], ACT.Gelu, bias=bn1c).then_inc(act_taken, 1)

            def front_soma(s, e):
                if s.tail and e == 0:
                    act.wait_ge(gs_ready, EH * s.n)
                act.wait_ge(act_filled, s.act("soma", e) + 1)
                act.activation(soma[1 - s.par][:, e, :], a_bank(s, "soma", e)[:], ACT.Gelu, bias=bsc[:, e:e + 1])\
                    .then_inc(act_taken, 1)

            def front_gate(s, e):
                if e == 0 and s.heavy and s.tail:
                    act.wait_ge(dve_taken, s.v0)
                act.wait_ge(act_filled, s.act("wg", e) + 1)
                act.activation(by_chunk_step(g[1 - s.par][:, e, :, :].rearrange("c b t -> c (b t)")), in_time(a_bank(s, "wg", e)[:]), ACT.Sigmoid, bias=bgc[:, e:e + 1])\
                    .then_inc(act_taken, 1)

            def y_turned(s):
                for e in range(EH):
                    act.wait_ge(act_filled, s.act("yT", e) + 1)
                    act.activation(yT[:, e, :], a_bank(s, "yT", e)[:], ACT.Copy).then_inc(act_taken, 1)

            def front_mod(s):
                if s.heavy and s.tail:
                    act.wait_ge(dve_filled, s.v0)
                act.wait_ge(act_filled, s.act("n2") + 1)
                act.activation(by_chunk_step(flat(mod[1 - s.par])), in_time(a_bank(s, "n2")[:]), ACT.Sigmoid, bias=bn2c)\
                    .then_inc(act_taken, 1)

            def mod_high(s):
                act.wait_ge(mod_ready, s.n + 2)
                act.activation(mods[1 - s.par][:, 0, :, :], mod[1 - s.par][:], ACT.Copy).then_inc(mods_high, 1)

            def x_high(s):
                act.wait_ge(xT_loaded, 16 * (s.n + 2))
                act.activation(xs[:, 0, :, :], xT[:], ACT.Copy).then_inc(xs_high, 1)

            def adapter_hidden(s):
                m = s.n - 1
                act.wait_ge(dve_filled, s.v0)
                act.wait_ge(act_filled, s.act("w1") + 1)
                for p in range(PAIRS):
                    for b in range(2):
                        half = slice(b * H, (b + 1) * H)
                        i = act.activation(hid[half, p, b * T:(b + 1) * T],
                                           a_bank(s, "w1")[half, p * P + b * T:p * P + (b + 1) * T], ACT.Relu,
                                           bias=b1g[half, bass.ds(m * SEQ + 2 * p + b, 1)])
                i.then_inc(act_taken, 1)

            def g_by_token(s):
                if s.heavy and s.tail:
                    act.wait_ge(dve_filled, s.v0)
                for h in range(2):
                    act.wait_ge(act_filled, s.act("gnat", h) + 1)
                    bank = a_bank(s, "gnat", h)[:].rearrange("t (i c) -> t i c", i=2)
                    for b in range(2):
                        half = slice(b * T, (b + 1) * T)
                        i = act.activation(gnat[1 - s.par][half, 2 * h:2 * h + 2, b, :], bank[half, :, :], ACT.Copy)
                    i.then_inc(act_taken, 1)

            def carried(s):
                if s is not FIRST:
                    act.wait_ge(dve_filled, s.v0)
                for k in range(1, NK):
                    act.wait_ge(act_filled, s.act("carry", k) + 1)
                    act.activation(carry[:, k, :], a_bank(s, "carry", k)[:, 0:E], ACT.Copy).then_inc(act_taken, 1)

            def one_pass(s):
                if s.front:
                    x_high(s)
                if s.tail:
                    temporal_gate(s)
                if s.front:
                    front_hidden(s)
                    front_soma(s, 0)
                    front_gate(s, 0)
                if s.tail:
                    y_turned(s)
                if s.tail:
                    adapter_hidden(s)
                if s.front:
                    front_mod(s)
                    front_gate(s, 1)
                    mod_high(s)
                    front_soma(s, 1)
                if s.front:
                    g_by_token(s)
                if s.heavy:
                    carried(s)

            act.wait_ge(const_loaded, 16 * CONST_LOADS)
            act.activation(alpha[:, 0:1], taud, ACT.Sigmoid, scale=-1.0).then_inc(act_const, 1)
            act.activation(alpha[:, 1:2], tauc, ACT.Sigmoid, scale=-1.0).then_inc(act_const, 1)
            for w, r in ((wgx, wgx_raw), (ws, ws_raw), (wn1, wn1_raw)):
                act.activation(w[:, 0, :, :], r, ACT.Copy).then_inc(act_const, 1)
            act.wait_ge(pe_const, 2 + NK - 1)
            for k in range(1, NK):
                act.activation(statepow[:, k - 1, :], abank[1][:, (k - 1) * P:k * P], ACT.Copy).then_inc(act_const, 1)
            act.wait_ge(pe_const, 2 + NK)
            act.activation(b1g[:], abank[2][:, 0:B], ACT.Copy).then_inc(act_const, 1)
            act.wait_ge(dve_const, DVE_MAX)
            for e in range(EH):
                act.activation(soma[1][:, e, 0:P], abank[0][:, e * P:(e + 1) * P], ACT.Exp, bias=smax[:, e:e + 1],
                               accum_out=ssum[:, e:e + 1]).then_inc(act_const, 1)
            act.wait_ge(dve_const, DVE_ALL)
            act.activation(lagw[:, 0, 0, :], bw, ACT.Copy).then_inc(act_const, 1)
            act.activation(lagw[:, 0, 1:LAGS, :], lagw_raw, ACT.Copy).then_inc(act_const, 1)
            act.wait_ge(pool_const, POOL_ALL)
            one_pass(FILL)
            one_pass(FIRST)
            one_pass(SECOND)
            with act.Fori(0, LOOPS) as j:
                for u in range(2):
                    one_pass(loop_pass(j, u))
            one_pass(SECOND_LAST)
            one_pass(LAST)
            one_pass(DRAIN)

        @block.gpsimd
        def _(pool):
            def rest(low, exact, high, done):
                pool.tensor_tensor(low, exact, high.bitcast(F32), ALU.subtract).then_inc(done, 1)

            def x_low(s):
                if s.n is not FILL.n:
                    pool.wait_ge(act_taken, s.a0)
                pool.wait_ge(xs_high, s.n + 2)
                rest(xs[:, 1, :, :], xT[:], xs[:, 0, :, :], xs_low)

            def mod_low(s):
                pool.wait_ge(mods_high, s.n + 2)
                rest(mods[1 - s.par][:, 1, :, :], mod[1 - s.par][:], mods[1 - s.par][:, 0, :, :], mods_low)

            def x_plus_beta(s):
                m = s.n - 1
                pool.wait_ge(xn_loaded, 16 * s.n)
                pool.wait_ge(y_ready, PAIRS * m)
                pool.tensor_tensor(xn[:], xn[:], bet0[:, None, :].to_broadcast([P, PAIRS, E]), ALU.add)\
                    .then_inc(xbeta_ready, 1)

            def add_lags(s, e, j0, j1):
                base = LAG_ADDS * s.n
                dst, t0 = temporal[s.par], e * (LAG_ADDS // 2)
                for j in range(max(j0, 1), j1):
                    slot = prod[:, prod_slot(e, j), :].rearrange("c (b t) -> c b t", b=SEQ)
                    pool.wait_ge(dve_taken, s.dve(f"lag{e}", j) + 1)
                    parts = [(dst[:, e, :, NK * j:T], slot[:, :, NK * j:T])]
                    if j < L // 2:
                        parts.append((dst[:, e, :, NK * (L - j):T], slot[:, :, 0:NK * j]))
                    for i, (to, frm) in enumerate(parts):
                        done = t0 + 2 * (j - 1) + i
                        if j > 1 or i or e:
                            pool.wait_ge(lags_added, base + done)
                        pool.tensor_tensor(to, to, frm, ALU.add).then_inc(lags_added, 1)

            def rstds(s, ve_, rstd_, done, steps, ready):
                m = s.n - 1
                for h in range(2):
                    pool.wait_ge(done, 2 * steps * m + steps * (h + 1))
                    pool.tensor_tensor(rstd_[:, 2 * h:2 * h + 2], ve_[:, 2 * h:2 * h + 2], minus_half[:, 0:2], ALU.pow)\
                        .then_inc(ready, 1)

            def y_sums(s):
                m = s.n - 1
                r = rows
                pool.wait_ge(rows_loaded, 16 * SEQ * s.n)
                pool.wait_ge(y_ready, PAIRS * s.n)
                pool.tensor_tensor(r[:, :, 0, :], y[:], r[:, :, 0, :], ALU.add).then_inc(yb_ready, 1)
                pool.tensor_tensor(r[:, :, 2, :], y[:], r[:, :, 2, :], ALU.add).then_inc(yb_ready, 1)

            def one_pass(s):
                if s.front:
                    x_low(s)
                if s.heavy:
                    add_lags(s, 0, 0, 5)
                if s.tail:
                    x_plus_beta(s)
                    rstds(s, ve, rstd, stats_done, 5, rstd_ready)
                if s.heavy:
                    add_lags(s, 0, 5, LAGS)
                if s.tail:
                    y_sums(s)
                if s.heavy:
                    add_lags(s, 1, 0, 5)
                if s.tail:
                    rstds(s, ve2, rstd2, stats2_done, 7, rstd2_ready)
                if s.front:
                    mod_low(s)
                if s.heavy:
                    add_lags(s, 1, 5, LAGS)

            pool.memset(ident[:], 0.0).then_inc(pool_const, 1)
            pool.wait_ge(pool_const, 1)
            pool.affine_select(out=ident[:], in_=ident[:], compare_op=ALU.not_equal, fill=1.0, base=0,
                               pattern=[[-1, P]], channel_multiplier=1).then_inc(pool_const, 1)
            pool.iota(lang_i[:], pattern=[[0, 1]], base=0, channel_multiplier=1).then_inc(pool_const, 1)
            for buf in (*gnat, hid, minus_half):
                pool.memset(buf[:], 0.0 if buf is not minus_half else -0.5).then_inc(pool_const, 1)
            pool.wait_ge(act_const, ACT_HIGH)
            for w, r in ((wgx, wgx_raw), (ws, ws_raw), (wn1, wn1_raw)):
                rest(w[:, 1, :, :], r, w[:, 0, :, :], pool_const)
            pool.wait_ge(act_const, ACT_SPLIT)
            rest(lagw[:, 1, 0, :], bw, lagw[:, 0, 0, :], pool_const)
            rest(lagw[:, 1, 1:LAGS, :], lagw_raw, lagw[:, 0, 1:LAGS, :], pool_const)
            pool.wait_ge(pool_const, POOL_SPLIT)
            one_pass(FILL)
            one_pass(FIRST)
            one_pass(SECOND)
            with pool.Fori(0, LOOPS) as j:
                for u in range(2):
                    one_pass(loop_pass(j, u))
            one_pass(SECOND_LAST)
            one_pass(LAST)
            one_pass(DRAIN)

        @block.vector
        def _(dve):
            def v_bank(s, name, k=0):
                return s.dve_bank(vbank, name, k)

            def context(s):
                dve.wait_ge(xT_loaded, 16 * (s.n + 2))
                for e in range(EH):
                    dve.tensor_tensor_scan(ctxT[:, e, :], decay[:], xT[:, e, :], 0.0, ALU.mult, ALU.add)\
                        .then_inc(ctx_ready, 1)

            def lag_products(s, e, j0, j1):
                for j in range(j0, j1):
                    name = f"lag{e}"
                    dve.wait_ge(dve_filled, s.dve(name, j) + 1)
                    bank = v_bank(s, name, j)[:].rearrange("c (b t) -> c b t", b=SEQ)
                    if j == 0:
                        to = temporal[s.par][:, e, :, :]
                    else:
                        to = prod[:, prod_slot(e, j), :].rearrange("c (b t) -> c b t", b=SEQ)
                        prod_free(s, e, j)
                    last = dve.tensor_tensor(to[:, :, NK * j:T], bank[:, :, NK * j:T], g[s.par][:, e, :, 0:T - NK * j], ALU.mult)
                    if 0 < j < L // 2:
                        last = dve.tensor_tensor(to[:, :, 0:NK * j], bank[:, :, 0:NK * j], g[s.par][:, e, :, 0:NK * j], ALU.mult)
                    last.then_inc(dve_taken, 1)

            def prod_free(s, e, j):
                i = e * (LAGS - 1) + j - 1 - PRODS
                before, i = (i < 0), i % (2 * (LAGS - 1))
                ei, ji = i // (LAGS - 1), i % (LAGS - 1) + 1
                if before and s is FIRST:
                    return
                adds = ei * (LAG_ADDS // 2) + min(2 * ji, LAG_ADDS // 2)
                dve.wait_ge(lags_added, LAG_ADDS * (s.n - before) + adds)

            def gated_soma(s):
                for e in range(EH):
                    dve.wait_ge(act_taken, s.act("temp", e) + 1)
                    dve.tensor_tensor(gs[:, e, :], gate[:, e, :], soma[1 - s.par][:, e, :], ALU.mult).then_inc(gs_ready, 1)

            def gated_x(s, e):
                dve.wait_ge(act_taken, s.act("wg", e) + 1)
                ge = by_chunk_step(g[1 - s.par][:, e, :, :].rearrange("c b t -> c (b t)"))
                dve.tensor_tensor(ge, in_time(xT[:, e, :]), ge, ALU.mult).then_inc(g_ready, 1)

            def front_mod(s):
                dve.wait_ge(act_taken, s.act("n2") + 1)
                dve.tensor_scalar(flat(mod[1 - s.par]), flat(mod[1 - s.par]), 0.5, None, ALU.add)\
                    .then_inc(mod_ready, 1)

            def decayed_mod(s):
                dve.wait_ge(dve_filled, s.dve("modnat") + 1)
                bank = v_bank(s, "modnat")
                for p in range(PAIRS):
                    i = dve.tensor_tensor(decmod[1 - s.par][:, p, :, :], bank[:, None, p * D:(p + 1) * D].to_broadcast([P, NK - 1, D]),
                                          statepow[:], ALU.mult)
                i.then_inc(dve_taken, 1)

            def norm_stats(src, h, st, mv_, ve_, done, before):
                for i in range(2):
                    dve.bn_stats(st[:, 2 * h + i, :], src[i]).then_inc(done, 1)
                dve.wait_ge(done, before + 2)
                dve.memset(waited[:], 0.0)
                for i in range(2):
                    dve.bn_aggr(mv_[:, 2 * h + i, :], st[:, 2 * h + i, :]).then_inc(done, 1)
                dve.wait_ge(done, before + 4)
                dve.tensor_scalar(ve_[:, 2 * h:2 * h + 2], mv_[:, 2 * h:2 * h + 2, 1], EPS, None, ALU.add).then_inc(done, 1)

            def first_norm(s):
                m = s.n - 1
                dve.wait_ge(rstd_ready, 2 * m)
                dve.wait_ge(yb_ready, 2 * m)
                dve.wait_ge(stored, 16 * m)
                dve.wait_ge(act_filled, s.a0)
                for h in range(2):
                    dve.wait_ge(dve_filled, s.dve("out", h) + 1)
                    bank = v_bank(s, "out", h)
                    src = [bank[:, i * E:(i + 1) * E] for i in range(2)]
                    norm_stats(src, h, stats, mv, ve, stats_done, 10 * m + 5 * h)
                    for i in range(2):
                        q = dve.scalar_tensor_tensor(y[:, 2 * h + i, :], src[i], mv[:, 2 * h + i, 0:1], gam0[:],
                                                     ALU.subtract, ALU.mult)
                    q.then_inc(dve_taken, 1)

            def first_residual(s):
                m = s.n - 1
                dve.wait_ge(dve_taken, s.dve("out", 1) + 1)
                dve.wait_ge(xbeta_ready, s.n)
                for p in range(PAIRS):
                    if p % 2 == 0:
                        dve.wait_ge(rstd_ready, 2 * m + 1 + p // 2)
                    dve.scalar_tensor_tensor(y[:, p, :], y[:, p, :], rstd[:, p:p + 1], xn[:, p, :],
                                             ALU.mult, ALU.add).then_inc(y_ready, 1)

            def second_norm(s, h):
                m = s.n - 1
                r = rows
                if h == 0:
                    dve.wait_ge(yb_ready, 2 * s.n)
                    dve.wait_ge(rstd2_ready, 2 * m)
                two = slice(2 * h, 2 * h + 2)
                dve.wait_ge(dve_filled, s.dve("w2", h) + 1)
                dve.tensor_tensor(z[:, two, :], v_bank(s, "w2", h)[:].rearrange("t (i c) -> t i c", i=2), r[:, two, 0, :],
                                  ALU.add).then_inc(dve_taken, 1)
                dve.wait_ge(dve_taken, s.dve("w2", h) + 1)
                norm_stats([z[:, 2 * h + i, :] for i in range(2)], h, stats2, mv2, ve2, stats2_done, 14 * m + 7 * h)
                for i in range(2):
                    p = 2 * h + i
                    q = dve.scalar_tensor_tensor(z[:, p, :], z[:, p, :], mv2[:, p, 0:1], r[:, p, 1, :],
                                                 ALU.subtract, ALU.mult)
                    q.then_inc(stats2_done, 1)

            def second_residual(s):
                m = s.n - 1
                for p in range(PAIRS):
                    dve.wait_ge(stats2_done, 14 * m + 7 * (p // 2) + 6 + p % 2)
                    if p % 2 == 0:
                        dve.wait_ge(rstd2_ready, 2 * m + 1 + p // 2)
                    dve.scalar_tensor_tensor(z[:, p, :], z[:, p, :], rstd2[:, p:p + 1], rows[:, p, 2, :],
                                             ALU.mult, ALU.add).then_inc(out_ready, 1)

            def blended_states(s, k):
                if k > 2:
                    dve.wait_ge(act_filled, s.act("carry", k - 2) + 1)
                elif s is not FIRST:
                    dve.wait_ge(act_filled, s.a0)
                for p in range(PAIRS):
                    dve.wait_ge(dve_filled, s.dve(f"state{k}", p) + 1)
                    dve.tensor_tensor(state[:, k % 2, p, :].rearrange("d (b c) -> d b c", b=2),
                                      v_bank(s, f"state{k}", p)[:].rearrange("d (b c) -> d b c", b=2),
                                      bw[:, None, :].to_broadcast([P, 2, E]), ALU.mult).then_inc(dve_taken, 1)

            def add_carried(s):
                dve.wait_ge(lags_added, LAG_ADDS * (s.n + 1))
                for k in range(1, NK):
                    dve.wait_ge(dve_filled, s.dve("carryT", k) + 1)
                    to = temporal[s.par][:].rearrange("c e b (p k) -> c e (b p) k", k=NK)[:, :, :, k]
                    dve.tensor_tensor(to, to, v_bank(s, "carryT", k)[:, 0:EH * P].rearrange("c (e r) -> c e r", e=EH),
                                      ALU.add).then_inc(dve_taken, 1)

            def one_pass(s):
                def lags(e, j0, j1):
                    if s.heavy:
                        lag_products(s, e, j0, j1)

                lags(0, 0, 3)
                if s.front:
                    context(s)
                if s.tail:
                    gated_soma(s)
                lags(0, 3, 5)
                if s.tail:
                    first_norm(s)
                lags(0, 5, 7)
                if s.tail:
                    first_residual(s)
                lags(0, 7, LAGS)
                lags(1, 0, 2)
                if s.front:
                    gated_x(s, 0)
                lags(1, 2, 4)
                if s.front:
                    front_mod(s)
                if s.tail:
                    second_norm(s, 0)
                lags(1, 4, 6)
                if s.front:
                    gated_x(s, 1)
                if s.tail:
                    second_norm(s, 1)
                lags(1, 6, LAGS)
                if s.heavy:
                    blended_states(s, 1)
                if s.tail:
                    second_residual(s)
                if s.heavy:
                    blended_states(s, 2)
                if s.front:
                    decayed_mod(s)
                if s.heavy:
                    blended_states(s, 3)
                    add_carried(s)

            count = [0]

            def step(instruction):
                count[0] += 1
                instruction.then_inc(dve_const, 1)
                dve.wait_ge(dve_const, count[0])

            dve.wait_ge(act_const, 2)
            dve.wait_ge(pool_const, 3)
            a = alpha[:, 0:1]
            step(dve.tensor_copy(powsq[:, 0:1], a))
            for i in range(1, 6):
                step(dve.tensor_tensor(powsq[:, i:i + 1], powsq[:, i - 1:i], powsq[:, i - 1:i], ALU.mult))
            step(dve.memset(revpow[:, T - 1:T], 1.0))
            for i in range(6):
                m = 1 << i
                step(dve.tensor_scalar(revpow[:, T - 2 * m:T - m], revpow[:, T - m:T], powsq[:, i:i + 1], None, ALU.mult))
            step(dve.memset(carrypow[:], 0.0))
            step(dve.tensor_copy(carrypow[:, L:L + 1], a))
            for i in range(4):
                m = 1 << i
                step(dve.tensor_scalar(carrypow[:, L + m:L + 2 * m], carrypow[:, L:L + m], powsq[:, i:i + 1], None, ALU.mult))
            step(dve.memset(statepow_t, 0.0))
            for k in range(1, NK):
                for b in range(2):
                    row = statepow_t[:, k - 1, b * T:(b + 1) * T].rearrange("d (p q) -> d q p", q=NK)
                    step(dve.tensor_copy(row[:, 0:k, :], revpow[:, T - k * L:T].rearrange("d (q p) -> d q p", p=L)))
            step(dve.memset(decay[:], 1.0))
            step(dve.tensor_scalar(decay[:], decay[:], alpha[:, 1:2], None, ALU.mult))
            step(dve.memset(decay[:].rearrange("c (b t) -> c b t", t=T)[:, :, 0:1], 0.0))
            step(dve.tensor_copy(lang[:], lang_i[:]))
            step(dve.tensor_copy(idf[:], ids_l[:]))
            step(dve.tensor_scalar(onehot[:], idf[:], lang[:], None, ALU.is_equal))
            assert count[0] == DVE_TABLES, count
            dve.wait_ge(pe_const, 2)
            step(dve.tensor_reduce(smax[:], abank[0][:, 0:EH * P].rearrange("c (e d) -> c e d", e=EH), AX.X, ALU.max))
            step(dve.tensor_scalar(smax[:], smax[:], -1.0, None, ALU.mult))
            assert count[0] == DVE_MAX, count
            dve.wait_ge(act_const, ACT_ALL)
            step(dve.reciprocal(srec[:], ssum[:]))
            for e in range(EH):
                step(dve.tensor_scalar(soma[0][:, e, 0:P], soma[1][:, e, 0:P], srec[:, e:e + 1], None, ALU.mult))
            assert count[0] == DVE_SOFTMAX, count
            dve.wait_ge(pe_const, PE_ALL)
            step(dve.tensor_copy(bw, abank[3][:, 0:E]))
            lags = [bw] + [lagw_raw[:, j, :] for j in range(LAGS - 1)] + [lagw_far[:, j, :] for j in range(L - LAGS)]
            for before, after in zip(lags, lags[1:]):
                step(dve.tensor_scalar(after, before, a, None, ALU.mult))
            assert count[0] == DVE_ALL, count
            dve.wait_ge(pool_const, POOL_SPLIT)
            one_pass(FILL)
            one_pass(FIRST)
            one_pass(SECOND)
            with dve.Fori(0, LOOPS) as j:
                for u in range(2):
                    one_pass(loop_pass(j, u))
            one_pass(SECOND_LAST)
            one_pass(LAST)
            one_pass(DRAIN)


def kernel(x, condB_tauraws, cond_256, condB_bn2, cond_1024, itok_B_0_8, L0_cond_tau_ctx, L0_cond_Wg, L0_cond_bg,
           L0_cond_Wn1, L0_cond_bn1, L0_cond_Wsoma, L0_cond_bsoma, L0_cond_Wtemp, L0_cond_btemp, L0_cond_Wout,
           L0_cond_gamma, L0_cond_beta, L1_cond_W1, L1_cond_b1, L1_cond_W2, L1_cond_b2, L1_cond_gamma, L1_cond_beta):
    import numpy as np
    import concourse.bacc as bacc
    from concourse.bass_utils import run_bass_kernel_spmd

    def turned(a):
        return np.ascontiguousarray(np.asarray(a).T)

    rows = np.asarray(x).reshape(B * T, E)
    inputs = [
        ("xT", turned(rows)), ("x", rows), ("tau", condB_tauraws), ("wn2T", turned(cond_256)), ("bn2", condB_bn2),
        ("blend", cond_1024), ("ids", np.asarray(itok_B_0_8).reshape(1, B)),
        ("tauc", np.asarray(L0_cond_tau_ctx).reshape(1, 1)), ("wgT", turned(L0_cond_Wg)), ("bg", L0_cond_bg),
        ("wn1T", turned(L0_cond_Wn1)), ("bn1", L0_cond_bn1), ("wsT", turned(L0_cond_Wsoma)), ("bs", L0_cond_bsoma),
        ("wtT", turned(L0_cond_Wtemp)), ("bt", L0_cond_btemp), ("woT", turned(L0_cond_Wout)),
        ("gamma", L0_cond_gamma), ("beta", L0_cond_beta), ("w1", L1_cond_W1), ("b1", L1_cond_b1), ("w2", L1_cond_W2),
        ("rows", np.concatenate([np.asarray(a) for a in (L1_cond_b2, L1_cond_gamma, L1_cond_beta)], axis=1)),
    ]
    nc = bacc.Bacc("TRN2", target_bir_lowering=False, num_devices=1)
    arrays, args = {}, []
    for name, a in inputs:
        a = np.ascontiguousarray(a)
        arrays[f"in_{name}"] = a
        args.append(nc.dram_tensor(f"in_{name}", a.shape, mybir.dt.from_np(a.dtype), kind="ExternalInput").ap())
    out = nc.dram_tensor("out_dram", (B * T, E), F32, kind="ExternalOutput").ap()
    build(nc, *args, out)
    r = run_bass_kernel_spmd(nc, [arrays], core_ids=[0])
    return r.results[0]["out_dram"].reshape(B, T, E)
```

```python
from contextlib import ExitStack

import concourse.bass as bass
from concourse import mybir

F32 = mybir.dt.float32
F32R = mybir.dt.float32r
I32 = mybir.dt.int32
ALU = mybir.AluOpType
ACT = mybir.ActivationFunctionType
AX = mybir.AxisListType

P = 128
B, T, E, D = 128, 64, 256, 128
H = 64
L = 16
NK = T // L
SEQ = 8
TOK = SEQ * T
TILES = B // SEQ
PAIRS = SEQ // 2
EH = E // P
LAGS = L // 2 + 1
PARTS = P // 2 // L
EPS = 1e-5
RING = 4


def fills(text):
    listed = []
    for name, ks in (word.split(":") for word in text.split()):
        first, _, last = ks.partition("-")
        listed += [(name, k) for k in range(int(first), int(last or first) + 1)]
    return listed


ACT_FILLS = fills("""
    temp:0-1 modrows:0-1 n1:0 modrows:2 grows:0-4 n2:0 grows:5 yT:0-1 w1:0 carry:0 soma:0-1 carry:1
""")
DVE_FILLS = fills("""
    lag0:0-7 out:0-1 lag0:8 lag1:0-1 wg:0 chunk0:0-1 lag1:2 chunk0:2-3 lag1:3 chunk1:0-3 lag1:4-6 w2:0
    chunk2:0-3 w2:1 wg:1 chunk3:0-2 lag1:7 chunk3:3 lag1:8 carryT:0-1
""")
TAIL_FILLS, FRONT_FILLS = ("temp", "out", "yT", "w1", "w2"), ("n1", "n2", "wg", "soma")


class Pass:

    def __init__(self, n, par, act_before, dve_before, phases=None, heavy=True, tail=True, front=True):
        self.n, self.par, self.heavy, self.tail, self.front = n, par, heavy, tail, front

        def here(name):
            return tail if name in TAIL_FILLS else front if name in FRONT_FILLS else heavy

        self.a_order = [f for f in ACT_FILLS if here(f[0])]
        self.v_order = [f for f in DVE_FILLS if here(f[0])]
        self.a0, self.v0 = act_before, dve_before
        self.phases = phases or (act_before % RING, dve_before % RING)

    def act(self, name, k=0):
        return self.a0 + self.a_order.index((name, k))

    def dve(self, name, k=0):
        return self.v0 + self.v_order.index((name, k))

    def act_bank(self, banks, name, k=0):
        return banks[(self.phases[0] + self.a_order.index((name, k))) % RING]

    def dve_bank(self, banks, name, k=0):
        return banks[(self.phases[1] + self.v_order.index((name, k))) % RING]

    def next_act(self):
        return self.a0 + len(self.a_order)

    def next_dve(self):
        return self.v0 + len(self.v_order)


FILL = Pass(-1, 1, 0, 0, heavy=False, tail=False)
FIRST = Pass(0, 0, FILL.next_act(), FILL.next_dve(), tail=False)
SECOND = FULL = Pass(1, 1, FIRST.next_act(), FIRST.next_dve())
FULL_ACT, FULL_DVE = len(FULL.a_order), len(FULL.v_order)
assert 2 * FULL_ACT % RING == 0 and 2 * FULL_DVE % RING == 0


def loop_pass(j, u):
    a, v = SECOND.next_act() + FULL_ACT * u, SECOND.next_dve() + FULL_DVE * u
    return Pass(2 * j + u + 2, u, 2 * FULL_ACT * j + a, 2 * FULL_DVE * j + v, (a % RING, v % RING))


LOOPS = (TILES - 4) // 2
SECOND_LAST = Pass(TILES - 2, 0, FULL.a0 + FULL_ACT * (TILES - 3), FULL.v0 + FULL_DVE * (TILES - 3))
LAST = Pass(TILES - 1, 1, SECOND_LAST.next_act(), SECOND_LAST.next_dve(), front=False)
DRAIN = Pass(TILES, 0, LAST.next_act(), LAST.next_dve(), heavy=False, front=False)

POOL_ZEROS, POOL_LAGS, POOL_ALL = 10, 20, 22
PE_TURNED, PE_BLEND, PE_ALL = EH, 2 * EH, 2 * EH + 1
ACT_ALPHA, ACT_EXP, ACT_WEIGHTS, ACT_ALL = 2, 4, 8, 11
DVE_MAX, DVE_POWERS, DVE_SUMS, DVE_SOFTMAX, DVE_WEIGHTS, DVE_LAGS, DVE_ALL = 5, 23, 25, 28, 31, 35, 39


def prod_slot(e, j):
    return (e * (LAGS - 1) + j - 1) % PRODS


PRODS = 4


def build(nc, xT_d, x_d, cols_d, wn2T_d, blend_d, ids_d, wgT_d, wn1T_d, wsT_d, wtT_d, woT_d, gamma_d, beta_d,
          w1_d, b1_d, w2_d, rows_d, out_d):
    NL = w1_d.shape[0]
    ctx = ExitStack()
    with ctx:
        def sb(name, shape, dt=F32):
            return ctx.enter_context(nc.sbuf_tensor(name, shape, dt))

        def sem(name):
            return ctx.enter_context(nc.semaphore(name))

        ident = sb("ident", [P, P])
        identr = sb("identr", [P, P], F32R)
        wg = sb("wg", [P, 2, 2, EH, E], F32R)
        wn1 = sb("wn1", [P, 2, EH, H], F32R)
        ws = sb("ws", [P, 2, EH, E], F32R)
        wn2 = sb("wn2", [H, D])
        wt = sb("wt", [P, 2, EH, E], F32R)
        wo = sb("wo", [P, 2, EH, E], F32R)
        cols = sb("cols", [P, 10])
        bgc, bsc, btc = (cols[:, 2 * i:2 * i + 2] for i in range(3))
        bn1c, bn2c = cols[0:H, 6:7], cols[:, 7:8]
        tauc = cols[:, 8:9]
        taud = cols[:, 9:10]
        alpha = sb("alpha", [P, 2])
        gam0 = sb("gam0", [P, E])
        bet0 = sb("bet0", [P, E])
        bw = sb("bw", [P, E])[:]
        lagw = sb("lagw", [P, 2, LAGS, E], F32R)
        lagw_far = sb("lagw_far", [P, L - LAGS, E])
        revpow = sb("revpow", [P, L])
        pows = sb("pows", [P, 1 + NK * L])
        powsq = sb("powsq", [P, 8])
        carrypow = sb("carrypow", [P, 3 * L])
        carrypow2 = sb("carrypow2", [P, NK - 1, 2 * L])
        decay = sb("decay", [P, TOK])
        ids = sb("ids", [1, B], I32)
        lang_i = sb("lang_i", [NL, 1], I32)
        lang = sb("lang", [NL, 1])
        b1g = sb("b1g", [P, B])
        smax = sb("smax", [P, EH])
        ssum = sb("ssum", [P, EH])
        srec = sb("srec", [P, EH])
        waited = sb("waited", [1, 1])
        minus_half = sb("minus_half", [P, PAIRS])

        xT = sb("xT", [P, EH, TOK])
        xs = sb("xs", [P, 2, EH, SEQ, 1 + T], F32R)
        xn = sb("xn", [P, PAIRS, E])
        rows = sb("rows", [P, PAIRS, 3, E])
        w1 = sb("w1", [P, PAIRS, EH, 2 * H])
        w2 = sb("w2", [P, PAIRS, E])
        wg_in = sb("wg_in", [P, TOK])
        h1 = wg_in[0:H, :]
        soma = [sb(f"soma{i}", [P, EH, TOK]) for i in range(2)]
        g = [sb(f"g{i}", [P, EH, SEQ, T]) for i in range(2)]
        mod = [sb(f"mod{i}", [P, SEQ, T]) for i in range(2)]
        mods = [sb(f"mods{i}", [P, 2, SEQ, T], F32R) for i in range(2)]
        temporal = [sb(f"temporal{i}", [P, EH, SEQ, T]) for i in range(2)]
        decmod = sb("decmod", [P, SEQ, L, NK - 1])
        modparts = sb("modparts", [P, NK - 1, SEQ, PARTS, L], F32R)
        gparts = sb("gparts", [P, EH, NK - 1, SEQ, PARTS, L], F32R)
        modrows = sb("modrows", [P, NK - 1, PAIRS, D], F32R)
        grows = sb("grows", [P, NK - 1, PAIRS, E], F32R)
        prod = sb("prod", [P, PRODS, TOK])
        lagw_raw = prod[:].rearrange("d s t -> d (s t)").rearrange("d (j c) -> d j c", c=E)
        blended = sb("blended", [P, 2, 2, NK - 1, E])
        raw = blended[:].rearrange("c a b j e -> c (a b j e)")
        wg_raw = raw[:, 0:2 * EH * E].rearrange("c (a k e) -> c a k e", a=2, e=E)
        ws_raw = raw[:, 2 * EH * E:3 * EH * E].rearrange("c (k e) -> c k e", e=E)
        wn1_raw = raw[:, 3 * EH * E:3 * EH * E + EH * H].rearrange("c (k e) -> c k e", e=H)
        carry = sb("carry", [P, NK - 1, E])
        gate = sb("gate", [P, EH, TOK])
        tgs = sb("tgs", [P, 2, EH, TOK], F32R)
        wt_raw, wo_raw = (gate[:, k, :].rearrange("c (k e) -> c k e", e=E) for k in range(2))
        y = sb("y", [P, PAIRS, E])
        ids_l = y[0:NL, 0, 0:B].bitcast(I32)
        idf, onehot, b1d = y[0:NL, 1, 0:B], y[0:NL, 2, 0:B], y[0:NL, 3, 0:2 * H]
        z = y
        gs = gate
        yT = gs
        hid = sb("hid", [P, PAIRS, P])
        stats = sb("stats", [P, PAIRS, 6])
        mv = sb("mv", [P, PAIRS, 2])
        ve = sb("ve", [P, PAIRS])
        rstd = sb("rstd", [P, PAIRS])
        stats2 = sb("stats2", [P, PAIRS, 6])
        mv2 = sb("mv2", [P, PAIRS, 2])
        ve2 = sb("ve2", [P, PAIRS])
        rstd2 = sb("rstd2", [P, PAIRS])

        abank = [ctx.enter_context(nc.psum_tensor(f"abank{i}", [P, 512], F32)) for i in range(RING)]
        vbank = [ctx.enter_context(nc.psum_tensor(f"vbank{i}", [P, 512], F32)) for i in range(RING)]

        act_filled = sem("act_filled")
        act_taken = sem("act_taken")
        dve_filled = sem("dve_filled")
        dve_taken = sem("dve_taken")
        cols_loaded = sem("cols_loaded")
        weights_loaded = sem("weights_loaded")
        blend_loaded = sem("blend_loaded")
        const_loaded = sem("const_loaded")
        ids_loaded = sem("ids_loaded")
        pool_const = sem("pool_const")
        dve_const = sem("dve_const")
        act_const = sem("act_const")
        pe_const = sem("pe_const")
        xT_loaded = sem("xT_loaded")
        xn_loaded = sem("xn_loaded")
        rows_loaded = sem("rows_loaded")
        w1_loaded = sem("w1_loaded")
        w2_loaded = sem("w2_loaded")
        xs_high = sem("xs_high")
        xs_low = sem("xs_low")
        mods_high = sem("mods_high")
        tgs_high = sem("tgs_high")
        sum_low = sem("sum_low")
        gs_low = sem("gs_low")
        mods_low = sem("mods_low")
        decmod_ready = sem("decmod_ready")
        parts_high = sem("parts_high")
        parts_low = sem("parts_low")
        wg_ready = sem("wg_ready")
        g_ready = sem("g_ready")
        gs_ready = sem("gs_ready")
        mod_ready = sem("mod_ready")
        lags_added = sem("lags_added")
        xbeta_ready = sem("xbeta_ready")
        stats_done = sem("stats_done")
        rstd_ready = sem("rstd_ready")
        y_ready = sem("y_ready")
        yb_ready = sem("yb_ready")
        stats2_done = sem("stats2_done")
        rstd2_ready = sem("rstd2_ready")
        out_ready = sem("out_ready")
        stored = sem("stored")

        LAG_ADDS = 2 * (2 * (LAGS - 2) + 1)

        def by_chunk_step(ap):
            return ap.rearrange("c (b p k) -> c b k p", b=SEQ, k=NK)

        def in_time(ap):
            return ap.rearrange("c (b k p) -> c b k p", b=SEQ, k=NK)

        def steps_of(ap):
            return ap.rearrange("c j b p -> c b p j")

        def chunks_of(ap):
            return ap.rearrange("c b (p k) -> c b p k", k=NK)[:, :, :, 0:NK - 1]

        def flat(ap):
            return ap.rearrange("d b t -> d (b t)")

        def pair_rows(dram, n):
            return dram[bass.ds(n * TOK, TOK), :].rearrange("(p t) c -> t p c", p=PAIRS)

        block = ctx.enter_context(nc.Block())

        WEIGHT_LOADS, CONST_LOADS = 4, 7

        @block.sync
        def _(sp):
            def load_xT(n):
                sp.dma_start(xT[:], xT_d[:, bass.ds(n * TOK, TOK)].rearrange("(k p) t -> p k t", p=P))\
                    .then_inc(xT_loaded, 16)

            def language(n, q):
                return sp.value_load(ids[0:1, bass.ds(n * SEQ + q, 1)], min_val=0, max_val=NL - 1)

            def load_down(n):
                for q in range(SEQ):
                    sp.dma_start(w1[:, q // 2, :, (q % 2) * H:(q % 2 + 1) * H],
                                 w1_d[bass.ds(language(n, q), 1), :, :].rearrange("l (k c) a -> c (l k) a", k=EH))\
                        .then_inc(w1_loaded, 16)

            def load_up(n):
                for q in range(SEQ):
                    lang_q = language(n, q)
                    half = slice((q % 2) * T, (q % 2 + 1) * T)
                    sp.dma_start(rows[half, q // 2, :, :].rearrange("t r c -> t (r c)"),
                                 rows_d[bass.ds(lang_q, 1), :].to_broadcast([T, 3 * E]))\
                        .then_inc(rows_loaded, 16)
                    sp.dma_start(w2[half, q // 2, :], w2_d[bass.ds(lang_q, 1), :, :].rearrange("l a c -> (l a) c"))\
                        .then_inc(w2_loaded, 16)

            sp.dma_start(cols[:], cols_d).then_inc(cols_loaded, 16)
            load_xT(0)
            for w, src in ((wg_raw, wgT_d.rearrange("(a k c) e -> c a k e", a=2, c=P)),
                           (ws_raw, wsT_d.rearrange("(k c) e -> c k e", c=P)),
                           (wn1_raw, wn1T_d.rearrange("(k c) e -> c k e", c=P)), (wn2[:], wn2T_d)):
                sp.dma_start(w, src).then_inc(weights_loaded, 16)
            sp.dma_start(ids[:], ids_d).then_inc(ids_loaded, 16)
            sp.dma_start(ids_l, ids_d.to_broadcast([NL, B])).then_inc(const_loaded, 16)
            for h in range(2):
                sp.dma_start(b1d[:, h * H:(h + 1) * H], b1_d).then_inc(const_loaded, 16)
            for w, src in ((wt_raw, wtT_d), (wo_raw, woT_d)):
                sp.dma_start(w, src.rearrange("(k c) e -> c k e", c=P)).then_inc(const_loaded, 16)
            for w, src in ((gam0, gamma_d), (bet0, beta_d)):
                sp.dma_start(w[:], src.rearrange("(a c) -> a c", a=1).to_broadcast([P, E])).then_inc(const_loaded, 16)
            sp.wait_ge(ids_loaded, 16)

            def one_pass(s):
                n = s.n
                if s.tail:
                    sp.wait_ge(y_ready, PAIRS * n)
                if s.heavy:
                    sp.dma_start(xn[:], pair_rows(x_d, n)).then_inc(xn_loaded, 16)
                if s.heavy and s.tail:
                    sp.wait_ge(act_filled, s.act("w1") + 1)
                if s.heavy:
                    load_down(n)
                if s.front and s is not SECOND_LAST:
                    sp.wait_ge(g_ready, EH * (n + 2))
                    load_xT(n + 2)
                if s.tail:
                    sp.wait_ge(out_ready, PAIRS * n)
                    sp.dma_start(pair_rows(out_d, n - 1), z[:]).then_inc(stored, 16)
                if s.heavy:
                    load_up(n)

            one_pass(FILL)
            one_pass(FIRST)
            one_pass(SECOND)
            with sp.Fori(0, LOOPS) as j:
                for u in range(2):
                    one_pass(loop_pass(j, u))
            one_pass(SECOND_LAST)
            one_pass(LAST)
            one_pass(DRAIN)
            sp.wait_ge(stored, 16 * TILES)

        @block.tensor
        def _(pe):
            def fill_act(use):
                if not isinstance(use, int) or use >= RING:
                    pe.wait_ge(act_taken, use - (RING - 1))

            def fill_dve(use):
                if not isinstance(use, int) or use >= RING:
                    pe.wait_ge(dve_taken, use - (RING - 1))

            def a_bank(s, name, k=0):
                return s.act_bank(abank, name, k)

            def v_bank(s, name, k=0):
                return s.dve_bank(vbank, name, k)

            def split_matmul(out, w, x, start=True, stop=True):
                for i, (a, b) in enumerate(((0, 1), (1, 0), (0, 0))):
                    last = pe.matmul(out, w(a), x(b), start=start and i == 0, stop=stop and i == 2)
                return last

            def split_dense(bank, w, x, e, width=P, m=P):
                for k in range(EH):
                    last = split_matmul(bank[0:m, :], lambda a: w[:, a, k, e * P:e * P + width], lambda a: x(a, k),
                                        k == 0, k == EH - 1)
                return last

            def x_parts(a, k):
                return xs[:, a, k, :, 1:]

            def lag_banks(s, e, j0, j1):
                for j in range(j0, j1):
                    lag_bank(s, e, j)

            def lag_bank(s, e, j):
                name = f"lag{e}"
                if e == 0 and j == 0:
                    pe.wait_ge(mod_ready, s.n + 1)
                    pe.wait_ge(mods_high, s.n + 1)
                    pe.wait_ge(mods_low, s.n + 1)
                fill_dve(s.dve(name, j))
                bank = v_bank(s, name, j)[:].rearrange("c (b t) -> c b t", b=SEQ)
                m = mod[s.par]
                last = split_matmul(bank[:, :, NK * j:T], lambda a: lagw[:, a, j, e * P:(e + 1) * P],
                                    lambda a: mods[s.par][:, a, :, 0:NK * (L - j)])
                if 0 < j < L // 2:
                    last = pe.matmul(bank[:, :, 0:NK * j], lagw_far[:, L - j - LAGS, e * P:(e + 1) * P], m[:, :, 0:NK * j],
                                     start=True, stop=True)
                last.then_inc(dve_filled, 1)

            def front_gate(s, e):
                fill_dve(s.dve("wg", e))
                bank = v_bank(s, "wg", e)
                col = slice(e * P, (e + 1) * P)
                for k in range(EH):
                    split_matmul(bank[:], lambda a: wg[:, a, 1, k, col], lambda a: xs[:, a, k, :, 1:], k == 0, False)
                for k in range(EH):
                    last = split_matmul(bank[:], lambda a: wg[:, a, 0, k, col], lambda a: xs[:, a, k, :, 0:T], False, k == EH - 1)
                last.then_inc(dve_filled, 1)

            def front_n1(s):
                pe.wait_ge(xs_high, s.n + 2)
                pe.wait_ge(xs_low, s.n + 2)
                fill_act(s.act("n1"))
                split_dense(a_bank(s, "n1"), wn1, x_parts, 0, H, H).then_inc(act_filled, 1)

            def front_soma(s, e):
                fill_act(s.act("soma", e))
                split_dense(a_bank(s, "soma", e), ws, x_parts, e).then_inc(act_filled, 1)

            def front_mod(s):
                pe.wait_ge(act_taken, s.act("n1") + 1)
                fill_act(s.act("n2"))
                pe.matmul(a_bank(s, "n2")[:], wn2[:], h1, start=True, stop=True).then_inc(act_filled, 1)

            def mod_rows(s, j):
                if j == 0:
                    pe.wait_ge(parts_high, 6 * (s.n + 1))
                    pe.wait_ge(parts_low, 3 * (s.n + 1))
                fill_act(s.act("modrows", j))
                for p in range(PAIRS):
                    last = pe.transpose(a_bank(s, "modrows", j)[:, p * D:(p + 1) * D].bitcast(F32R),
                                        modparts[:, j, 2 * p:2 * p + 2, :, :].rearrange("d b r p -> d (b r p)"), identr[:])
                last.then_inc(act_filled, 1)

            def g_rows(s, i):
                fill_act(s.act("grows", i))
                for q in range(2):
                    for e in range(EH):
                        p = 2 * (i % 2) + q
                        last = pe.transpose(a_bank(s, "grows", i)[:, q * E + e * P:q * E + (e + 1) * P].bitcast(F32R),
                                            gparts[:, e, i // 2, 2 * p:2 * p + 2, :, :].rearrange("c b r p -> c (b r p)"), identr[:])
                last.then_inc(act_filled, 1)

            def tail_temporal(s, e):
                if e == 0:
                    if s is SECOND:
                        pe.wait_ge(pool_const, POOL_ALL)
                    pe.wait_ge(tgs_high, 4 * (s.n - 1) + 2)
                    pe.wait_ge(sum_low, 2 * s.n)
                fill_act(s.act("temp", e))
                split_dense(a_bank(s, "temp", e), wt, lambda a, k: tgs[:, a, k, :], e).then_inc(act_filled, 1)

            def tail_out(s, h):
                if h == 0:
                    pe.wait_ge(tgs_high, 4 * s.n)
                    pe.wait_ge(gs_low, 2 * s.n)
                fill_dve(s.dve("out", h))
                for i in range(2):
                    p = 2 * h + i
                    for k in range(EH):
                        last = split_matmul(v_bank(s, "out", h)[:, i * E:(i + 1) * E], lambda a: tgs[:, a, k, p * P:(p + 1) * P],
                                            lambda a: wo[:, a, k, :], k == 0, k == EH - 1)
                last.then_inc(dve_filled, 1)

            def tail_yT(s, e):
                if e == 0:
                    pe.wait_ge(y_ready, PAIRS * s.n)
                fill_act(s.act("yT", e))
                for p in range(PAIRS):
                    last = pe.transpose(a_bank(s, "yT", e)[:, p * P:(p + 1) * P], y[:, p, e * P:(e + 1) * P], ident[:])
                last.then_inc(act_filled, 1)

            def tail_w1(s):
                pe.wait_ge(act_taken, s.act("yT", 1) + 1)
                pe.wait_ge(w1_loaded, 16 * SEQ * s.n)
                fill_act(s.act("w1"))
                for p in range(PAIRS):
                    for k in range(EH):
                        last = pe.matmul(a_bank(s, "w1")[:, p * P:(p + 1) * P], w1[:, p, k, :],
                                         yT[:, k, p * P:(p + 1) * P], start=(k == 0), stop=(k == EH - 1))
                last.then_inc(act_filled, 1)

            def tail_w2(s, h):
                if h == 0:
                    pe.wait_ge(act_taken, s.act("w1") + 1)
                    pe.wait_ge(w2_loaded, 16 * SEQ * s.n)
                fill_dve(s.dve("w2", h))
                for i in range(2):
                    p = 2 * h + i
                    last = pe.matmul(v_bank(s, "w2", h)[:, i * E:(i + 1) * E], hid[:, p, :], w2[:, p, :],
                                     start=True, stop=True)
                last.then_inc(dve_filled, 1)

            def chunk_sums(s, p, i):
                if p == 0 and i == 0:
                    pe.wait_ge(act_taken, s.act("grows", 2 * (NK - 1) - 1) + 1)
                b = i % 2
                half = slice(b * P // 2, (b + 1) * P // 2)
                fill_dve(s.dve(f"chunk{p}", i))
                for j in (0, 1) if i < 2 else (2,):
                    last = pe.matmul(v_bank(s, f"chunk{p}", i)[:, j % 2 * E:(j % 2 + 1) * E], modrows[half, j, p, :],
                                     grows[half, j, p, :], start=True, stop=True)
                last.then_inc(dve_filled, 1)

            def carried(s, p):
                if p == 0:
                    fill_act(s.act("carry", 1))
                pe.wait_ge(dve_taken, s.dve(f"chunk{p}", 3) + 1)
                first, later = a_bank(s, "carry", 1), a_bank(s, "carry", p // 2)
                col = E * (p // 2)
                for b in range(2):
                    pe.matmul(first[2 * L * p:2 * L * (p + 1), 0:E], carrypow[:, L * (1 - b):L * (3 - b)],
                              blended[:, p % 2, b, 0, :], start=(b == 0), stop=(b == 1))
                for b in range(2):
                    to = later[2 * L * (2 * (p % 2) + b):2 * L * (2 * (p % 2) + b + 1), col:col + E]
                    for j in range(NK - 1):
                        last = pe.matmul(to, carrypow2[:, j, :], blended[:, p % 2, b, j, :],
                                         start=(j == 0), stop=(j == NK - 2))
                if p % 2 == 1:
                    last.then_inc(act_filled, 1)

            def carried_T(s, i):
                pe.wait_ge(act_taken, s.act("carry", i) + 1)
                fill_dve(s.dve("carryT", i))
                for k, t in enumerate((2,) if i == 0 else (0, 1)):
                    for e in range(EH):
                        last = pe.transpose(v_bank(s, "carryT", i)[:, k * E + e * P:k * E + (e + 1) * P],
                                            carry[:, t, e * P:(e + 1) * P], ident[:])
                last.then_inc(dve_filled, 1)

            def one_pass(s):
                def heavy(stage, *k):
                    if s.heavy:
                        stage(s, *k)

                def tail(stage, *k):
                    if s.tail:
                        stage(s, *k)

                def front(stage, *k):
                    if s.front:
                        stage(s, *k)

                heavy(lag_banks, 0, 0, 6)
                tail(tail_temporal, 0)
                tail(tail_temporal, 1)
                heavy(lag_banks, 0, 6, 7)
                heavy(mod_rows, 0)
                heavy(mod_rows, 1)
                heavy(lag_banks, 0, 7, 8)
                front(front_n1)
                tail(tail_out, 0)
                heavy(mod_rows, 2)
                heavy(g_rows, 0)
                heavy(g_rows, 1)
                tail(tail_out, 1)
                heavy(lag_banks, 0, 8, 9)
                heavy(g_rows, 2)
                heavy(lag_banks, 1, 0, 2)
                heavy(g_rows, 3)
                heavy(g_rows, 4)
                front(front_mod)
                heavy(g_rows, 5)
                front(front_gate, 0)
                for i in range(0, 2):
                    heavy(chunk_sums, 0, i)
                tail(tail_yT, 0)
                heavy(lag_banks, 1, 2, 3)
                heavy(chunk_sums, 0, 2)
                tail(tail_yT, 1)
                heavy(chunk_sums, 0, 3)
                heavy(lag_banks, 1, 3, 4)
                for i in range(0, 2):
                    heavy(chunk_sums, 1, i)
                tail(tail_w1)
                for i in range(2, 4):
                    heavy(chunk_sums, 1, i)
                heavy(lag_banks, 1, 4, 7)
                tail(tail_w2, 0)
                heavy(carried, 0)
                heavy(carried, 1)
                heavy(chunk_sums, 2, 0)
                front(front_soma, 0)
                for i in range(1, 4):
                    heavy(chunk_sums, 2, i)
                tail(tail_w2, 1)
                front(front_gate, 1)
                heavy(chunk_sums, 3, 0)
                front(front_soma, 1)
                for i in range(1, 3):
                    heavy(chunk_sums, 3, i)
                heavy(lag_banks, 1, 7, 8)
                heavy(chunk_sums, 3, 3)
                heavy(carried, 2)
                heavy(lag_banks, 1, 8, 9)
                heavy(carried, 3)
                heavy(carried_T, 0)
                heavy(carried_T, 1)

            pe.wait_ge(pool_const, 2)
            pe.wait_ge(blend_loaded, 16)
            for e in range(EH):
                pe.transpose(vbank[2][:, e * P:(e + 1) * P], bw[:, e * P:(e + 1) * P], ident[:]).then_inc(pe_const, 1)
            pe.wait_ge(dve_const, DVE_SOFTMAX)
            for e in range(EH):
                pe.transpose(vbank[3][:, e * P:(e + 1) * P], soma[1][:, e, 0:P], ident[:]).then_inc(pe_const, 1)
            pe.wait_ge(act_const, ACT_WEIGHTS)
            pe.wait_ge(dve_const, DVE_WEIGHTS)
            pe.wait_ge(weights_loaded, 16 * WEIGHT_LOADS)
            pe.wait_ge(pool_const, POOL_ZEROS)
            one_pass(FILL)
            pe.wait_ge(const_loaded, 16 * CONST_LOADS)
            pe.wait_ge(dve_const, DVE_ALL)
            pe.matmul(vbank[2][:, 0:B], b1d, onehot, start=True, stop=True).then_inc(pe_const, 1)
            pe.wait_ge(act_const, ACT_ALL)
            pe.wait_ge(pool_const, POOL_LAGS)
            one_pass(FIRST)
            one_pass(SECOND)
            with pe.Fori(0, LOOPS) as j:
                for u in range(2):
                    one_pass(loop_pass(j, u))
            one_pass(SECOND_LAST)
            one_pass(LAST)
            one_pass(DRAIN)

        @block.scalar
        def _(act):
            def a_bank(s, name, k=0):
                return s.act_bank(abank, name, k)

            def sum_high(s, e):
                if e == 0:
                    act.wait_ge(dve_taken, s.v0)
                    act.wait_ge(dve_filled, s.v0)
                act.activation(tgs[:, 0, e, :], flat(temporal[1 - s.par][:, e, :, :]), ACT.Copy).then_inc(tgs_high, 1)

            def gs_high(s, e):
                act.wait_ge(act_filled, s.act("temp", 1) + 1)
                act.wait_ge(gs_ready, EH * (s.n - 1) + e + 1)
                act.activation(tgs[:, 0, e, :], gs[:, e, :], ACT.Copy).then_inc(tgs_high, 1)

            def temporal_gate(s, e):
                if s is SECOND and e == 0:
                    act.wait_ge(pool_const, POOL_ALL)
                act.wait_ge(act_filled, s.act("temp", e) + 1)
                act.activation(in_time(gate[:, e, :]), by_chunk_step(a_bank(s, "temp", e)[:]),
                               ACT.Sigmoid, bias=btc[:, e:e + 1]).then_inc(act_taken, 1)

            def front_hidden(s):
                act.wait_ge(act_filled, s.act("n1") + 1)
                act.activation(h1, a_bank(s, "n1")[0:H, :], ACT.Gelu, bias=bn1c).then_inc(act_taken, 1)

            def front_soma(s, e):
                if s.tail and e == 0:
                    act.wait_ge(gs_ready, EH * s.n)
                act.wait_ge(act_filled, s.act("soma", e) + 1)
                act.activation(soma[1 - s.par][:, e, :], a_bank(s, "soma", e)[:], ACT.Gelu, bias=bsc[:, e:e + 1])\
                    .then_inc(act_taken, 1)

            def front_gate(s, e):
                if e == 0 and s.heavy and s.tail:
                    act.wait_ge(dve_taken, s.v0)
                act.wait_ge(dve_taken, s.dve("wg", e) + 1)
                act.activation(by_chunk_step(flat(g[1 - s.par][:, e, :, :])), in_time(wg_in[:]), ACT.Sigmoid, bias=bgc[:, e:e + 1])\
                    .then_inc(wg_ready, 1)

            def y_turned(s, e):
                act.wait_ge(act_filled, s.act("yT", e) + 1)
                act.activation(yT[:, e, :], a_bank(s, "yT", e)[:], ACT.Copy).then_inc(act_taken, 1)

            def front_mod(s):
                if s.heavy and s.tail:
                    act.wait_ge(dve_filled, s.v0)
                act.wait_ge(act_filled, s.act("n2") + 1)
                act.activation(by_chunk_step(flat(mod[1 - s.par][:])), in_time(a_bank(s, "n2")[:]), ACT.Sigmoid, bias=bn2c)\
                    .then_inc(act_taken, 1)

            def mod_high(s):
                act.wait_ge(act_taken, s.act("n2") + 1)
                act.activation(mod[1 - s.par][:], mod[1 - s.par][:], ACT.Copy, bias=0.5).then_inc(mod_ready, 1)
                act.wait_ge(mod_ready, s.n + 2)
                act.activation(mods[1 - s.par][:, 0, :, :], mod[1 - s.par][:], ACT.Copy).then_inc(mods_high, 1)

            def x_high(s):
                act.wait_ge(xT_loaded, 16 * (s.n + 2))
                act.activation(xs[:, 0, :, :, 1:], xT[:].rearrange("c k (b t) -> c k b t", b=SEQ), ACT.Copy).then_inc(xs_high, 1)

            def adapter_hidden(s):
                m = s.n - 1
                act.wait_ge(dve_filled, s.v0)
                act.wait_ge(act_filled, s.act("w1") + 1)
                for p in range(PAIRS):
                    for b in range(2):
                        half = slice(b * H, (b + 1) * H)
                        i = act.activation(hid[half, p, b * T:(b + 1) * T],
                                           a_bank(s, "w1")[half, p * P + b * T:p * P + (b + 1) * T], ACT.Relu,
                                           bias=b1g[half, bass.ds(m * SEQ + 2 * p + b, 1)])
                i.then_inc(act_taken, 1)

            def parts_rounded(s):
                act.wait_ge(g_ready, EH * (s.n + 1))
                act.wait_ge(decmod_ready, s.n + 1)
                for r in (0, 1):
                    act.activation(steps_of(modparts[:, :, :, r, :]), decmod[:], ACT.Copy).then_inc(parts_high, 1)
                for e in range(EH):
                    for r in (0, 2):
                        act.activation(steps_of(gparts[:, e, :, :, r, :]), chunks_of(g[s.par][:, e, :, :]), ACT.Copy)\
                            .then_inc(parts_high, 1)

            def mod_rows(s, j):
                if s is not FIRST and j == 0:
                    act.wait_ge(dve_filled, s.v0)
                act.wait_ge(act_filled, s.act("modrows", j) + 1)
                act.activation(modrows[:, j, :, :].rearrange("t a d -> t (a d)"), a_bank(s, "modrows", j)[:], ACT.Copy)\
                    .then_inc(act_taken, 1)

            def g_rows(s, i):
                act.wait_ge(act_filled, s.act("grows", i) + 1)
                act.activation(grows[:, i // 2, 2 * (i % 2):2 * (i % 2) + 2, :].rearrange("t a c -> t (a c)"),
                               a_bank(s, "grows", i)[:], ACT.Copy).then_inc(act_taken, 1)

            def carried(s, i):
                if s is not FIRST and i == 0:
                    act.wait_ge(dve_filled, s.v0)
                act.wait_ge(act_filled, s.act("carry", i) + 1)
                if i == 0:
                    act.activation(carry[:, 2, :], a_bank(s, "carry", 0)[:, 0:E], ACT.Copy).then_inc(act_taken, 1)
                else:
                    act.activation(carry[:, 0:2, :].rearrange("t a c -> t (a c)"), a_bank(s, "carry", 1)[:], ACT.Copy)\
                        .then_inc(act_taken, 1)

            def one_pass(s):
                def heavy(stage, *k):
                    if s.heavy:
                        stage(s, *k)

                def tail(stage, *k):
                    if s.tail:
                        stage(s, *k)

                def front(stage, *k):
                    if s.front:
                        stage(s, *k)

                tail(sum_high, 0)
                tail(sum_high, 1)
                heavy(parts_rounded)
                if s is not FILL:
                    front(x_high)
                tail(temporal_gate, 0)
                tail(temporal_gate, 1)
                tail(gs_high, 0)
                heavy(mod_rows, 0)
                tail(gs_high, 1)
                heavy(mod_rows, 1)
                front(front_hidden)
                heavy(mod_rows, 2)
                for i in range(0, 5):
                    heavy(g_rows, i)
                front(front_mod)
                heavy(g_rows, 5)
                tail(y_turned, 0)
                tail(y_turned, 1)
                front(front_gate, 0)
                front(mod_high)
                tail(adapter_hidden)
                heavy(carried, 0)
                front(front_soma, 0)
                front(front_soma, 1)
                front(front_gate, 1)
                heavy(carried, 1)

            act.dma_start(bw, blend_d).then_inc(blend_loaded, 16)
            act.wait_ge(cols_loaded, 16)
            act.activation(alpha[:, 0:1], taud, ACT.Sigmoid, scale=-1.0).then_inc(act_const, 1)
            act.activation(alpha[:, 1:2], tauc, ACT.Sigmoid, scale=-1.0).then_inc(act_const, 1)
            act.wait_ge(dve_const, DVE_MAX)
            for e in range(EH):
                act.activation(soma[1][:, e, 0:P], vbank[2][:, e * P:(e + 1) * P], ACT.Exp, bias=smax[:, e:e + 1],
                               accum_out=ssum[:, e:e + 1]).then_inc(act_const, 1)
            x_high(FILL)
            act.wait_ge(pool_const, 2)
            act.activation(identr[:], ident[:], ACT.Copy).then_inc(act_const, 1)
            act.wait_ge(weights_loaded, 16 * WEIGHT_LOADS)
            act.activation(ws[:, 0, :, :], ws_raw, ACT.Copy).then_inc(act_const, 1)
            act.activation(wn1[:, 0, :, :], wn1_raw, ACT.Copy).then_inc(act_const, 1)
            act.wait_ge(dve_const, DVE_SUMS)
            act.activation(wg[:, 0, :, :, :], wg_raw, ACT.Copy).then_inc(act_const, 1)
            one_pass(FILL)
            act.wait_ge(const_loaded, 16 * CONST_LOADS)
            act.activation(wt[:, 0, :, :], wt_raw, ACT.Copy).then_inc(act_const, 1)
            act.activation(wo[:, 0, :, :], wo_raw, ACT.Copy).then_inc(act_const, 1)
            act.wait_ge(pe_const, PE_ALL)
            act.activation(b1g[:], vbank[2][:, 0:B], ACT.Copy).then_inc(act_const, 1)
            act.wait_ge(pool_const, POOL_ZEROS)
            one_pass(FIRST)
            one_pass(SECOND)
            with act.Fori(0, LOOPS) as j:
                for u in range(2):
                    one_pass(loop_pass(j, u))
            one_pass(SECOND_LAST)
            one_pass(LAST)
            one_pass(DRAIN)

        @block.gpsimd
        def _(pool):
            def rest(low, exact, high, done):
                pool.tensor_tensor(low, exact, high.bitcast(F32), ALU.subtract).then_inc(done, 1)

            def x_low(s):
                if s.n is not FILL.n:
                    pool.wait_ge(act_taken, s.a0)
                pool.wait_ge(xs_high, s.n + 2)
                rest(xs[:, 1, :, :, 1:], xT[:].rearrange("c k (b t) -> c k b t", b=SEQ), xs[:, 0, :, :, 1:], xs_low)

            def sum_rest(s, e):
                pool.wait_ge(tgs_high, 4 * (s.n - 1) + e + 1)
                rest(tgs[:, 1, e, :], flat(temporal[1 - s.par][:, e, :, :]), tgs[:, 0, e, :], sum_low)

            def mod_low(s):
                pool.wait_ge(mods_high, s.n + 2)
                rest(mods[1 - s.par][:, 1, :, :], mod[1 - s.par][:], mods[1 - s.par][:, 0, :, :], mods_low)

            def x_plus_beta(s):
                m = s.n - 1
                pool.wait_ge(xn_loaded, 16 * s.n)
                pool.wait_ge(y_ready, PAIRS * m)
                pool.tensor_tensor(xn[:], xn[:], bet0[:, None, :].to_broadcast([P, PAIRS, E]), ALU.add)\
                    .then_inc(xbeta_ready, 1)

            def add_lags(s, e, j0, j1):
                base = LAG_ADDS * s.n
                dst, t0 = temporal[s.par], e * (LAG_ADDS // 2)
                for j in range(max(j0, 1), j1):
                    slot = prod[:, prod_slot(e, j), :].rearrange("c (b t) -> c b t", b=SEQ)
                    pool.wait_ge(dve_taken, s.dve(f"lag{e}", j) + 1)
                    parts = [(dst[:, e, :, NK * j:T], slot[:, :, NK * j:T])]
                    if j < L // 2:
                        parts.append((dst[:, e, :, NK * (L - j):T], slot[:, :, 0:NK * j]))
                    for i, (to, frm) in enumerate(parts):
                        done = t0 + 2 * (j - 1) + i
                        if j > 1 or i or e:
                            pool.wait_ge(lags_added, base + done)
                        pool.tensor_tensor(to, to, frm, ALU.add).then_inc(lags_added, 1)

            def first_rstd(s, h):
                pool.wait_ge(stats_done, 10 * (s.n - 1) + 5 * (h + 1))
                two = slice(2 * h, 2 * h + 2)
                pool.tensor_tensor(rstd[:, two], ve[:, two], minus_half[:, two], ALU.pow).then_inc(rstd_ready, 1)

            def second_rstd(s, h):
                pool.wait_ge(stats2_done, 14 * (s.n - 1) + 7 * (h + 1))
                two = slice(2 * h, 2 * h + 2)
                pool.tensor_tensor(rstd2[:, two], ve2[:, two], minus_half[:, two], ALU.pow).then_inc(rstd2_ready, 1)

            def y_sum(s, i):
                if i == 0:
                    pool.wait_ge(rows_loaded, 16 * SEQ * s.n)
                    pool.wait_ge(y_ready, PAIRS * s.n)
                pool.tensor_tensor(rows[:, :, 2 * i, :], y[:], rows[:, :, 2 * i, :], ALU.add).then_inc(yb_ready, 1)

            def one_pass(s):
                def heavy(stage, *k):
                    if s.heavy:
                        stage(s, *k)

                def tail(stage, *k):
                    if s.tail:
                        stage(s, *k)

                def front(stage, *k):
                    if s.front:
                        stage(s, *k)

                tail(sum_rest, 0)
                tail(sum_rest, 1)
                heavy(add_lags, 0, 1, 3)
                if s is not FILL:
                    front(x_low)
                heavy(add_lags, 0, 3, 6)
                tail(x_plus_beta)
                tail(first_rstd, 0)
                heavy(add_lags, 0, 6, 7)
                tail(first_rstd, 1)
                heavy(add_lags, 0, 7, 8)
                tail(y_sum, 0)
                heavy(add_lags, 0, 8, 9)
                heavy(add_lags, 1, 1, 3)
                tail(y_sum, 1)
                heavy(add_lags, 1, 3, 7)
                front(mod_low)
                tail(second_rstd, 0)
                heavy(add_lags, 1, 7, 9)
                tail(second_rstd, 1)

            pool.memset(ident[:], 0.0).then_inc(pool_const, 1)
            pool.wait_ge(pool_const, 1)
            pool.affine_select(out=ident[:], in_=ident[:], compare_op=ALU.not_equal, fill=1.0, base=0,
                               pattern=[[-1, P]], channel_multiplier=1).then_inc(pool_const, 1)
            pool.iota(lang_i[:], pattern=[[0, 1]], base=0, channel_multiplier=1).then_inc(pool_const, 1)
            pool.memset(hid[:], 0.0).then_inc(pool_const, 1)
            pool.memset(minus_half[:], -0.5).then_inc(pool_const, 1)
            pool.memset(modparts[:, :, :, PARTS - 1, :].bitcast(F32), 0.0).then_inc(pool_const, 1)
            for e in range(EH):
                pool.memset(gparts[:, e, :, :, PARTS - 1, :].bitcast(F32), 0.0).then_inc(pool_const, 1)
            for part in range(2):
                pool.memset(xs[:, part, :, :, 0:1].bitcast(F32), 0.0).then_inc(pool_const, 1)
            x_low(FILL)
            pool.memset(carrypow[:], 0.0).then_inc(pool_const, 1)
            pool.memset(carrypow2[:], 0.0).then_inc(pool_const, 1)
            pool.wait_ge(pool_const, POOL_ZEROS + 2)
            pool.wait_ge(dve_const, DVE_POWERS)
            pool.tensor_copy(carrypow[:, L:2 * L], pows[:, 1:L + 1]).then_inc(pool_const, 1)
            later = carrypow2[:].rearrange("d j (t k) -> d j k t", k=2)
            for j, k in ((0, 2), (0, 3), (1, 2), (1, 3), (2, 3)):
                first = L * (k - 1 - j) + 1
                pool.tensor_copy(later[:, j, k - 2, :], pows[:, first:first + L]).then_inc(pool_const, 1)
            pool.wait_ge(dve_const, DVE_LAGS)
            rest(lagw[:, 1, 0, :], bw, lagw[:, 0, 0, :], pool_const)
            rest(lagw[:, 1, 1:LAGS, :], lagw_raw, lagw[:, 0, 1:LAGS, :], pool_const)
            one_pass(FILL)
            pool.wait_ge(const_loaded, 16 * CONST_LOADS)
            pool.wait_ge(act_const, ACT_ALL - 1)
            rest(wt[:, 1, :, :], wt_raw, wt[:, 0, :, :], pool_const)
            rest(wo[:, 1, :, :], wo_raw, wo[:, 0, :, :], pool_const)
            one_pass(FIRST)
            one_pass(SECOND)
            with pool.Fori(0, LOOPS) as j:
                for u in range(2):
                    one_pass(loop_pass(j, u))
            one_pass(SECOND_LAST)
            one_pass(LAST)
            one_pass(DRAIN)

        @block.vector
        def _(dve):
            def v_bank(s, name, k=0):
                return s.dve_bank(vbank, name, k)

            def gate_scan(s, e):
                dve.wait_ge(dve_filled, s.dve("wg", e) + 1)
                if e == 0:
                    dve.wait_ge(act_filled, s.act("n2") + 1)
                else:
                    dve.wait_ge(wg_ready, EH * (s.n + 1) + e)
                dve.tensor_tensor_scan(wg_in[:], decay[:], v_bank(s, "wg", e)[:], 0.0, ALU.mult, ALU.add).then_inc(dve_taken, 1)

            def lag_products(s, e, j0, j1):
                if e == 0 and j0 == 0:
                    dve.wait_ge(g_ready, EH * (s.n + 1))
                    if s is not FIRST and s is not SECOND:
                        dve.wait_ge(sum_low, 2 * (s.n - 1))
                for j in range(j0, j1):
                    name = f"lag{e}"
                    dve.wait_ge(dve_filled, s.dve(name, j) + 1)
                    bank = v_bank(s, name, j)[:].rearrange("c (b t) -> c b t", b=SEQ)
                    if j == 0:
                        to = temporal[s.par][:, e, :, :]
                    else:
                        to = prod[:, prod_slot(e, j), :].rearrange("c (b t) -> c b t", b=SEQ)
                        prod_free(s, e, j)
                    last = dve.tensor_tensor(to[:, :, NK * j:T], bank[:, :, NK * j:T], g[s.par][:, e, :, 0:T - NK * j], ALU.mult)
                    if 0 < j < L // 2:
                        last = dve.tensor_tensor(to[:, :, 0:NK * j], bank[:, :, 0:NK * j], g[s.par][:, e, :, 0:NK * j], ALU.mult)
                    last.then_inc(dve_taken, 1)

            def prod_free(s, e, j):
                i = e * (LAGS - 1) + j - 1 - PRODS
                before, i = (i < 0), i % (2 * (LAGS - 1))
                ei, ji = i // (LAGS - 1), i % (LAGS - 1) + 1
                if before and s is FIRST:
                    return
                adds = ei * (LAG_ADDS // 2) + min(2 * ji, LAG_ADDS // 2)
                dve.wait_ge(lags_added, LAG_ADDS * (s.n - before) + adds)

            def gated_soma(s, e):
                dve.wait_ge(act_taken, s.act("temp", e) + 1)
                dve.tensor_tensor(gs[:, e, :], gate[:, e, :], soma[1 - s.par][:, e, :], ALU.mult).then_inc(gs_ready, 1)

            def gs_rest(s, e):
                dve.wait_ge(gs_ready, EH * (s.n - 1) + e + 1)
                dve.wait_ge(tgs_high, 4 * (s.n - 1) + 3 + e)
                dve.tensor_tensor(tgs[:, 1, e, :], gs[:, e, :], tgs[:, 0, e, :].bitcast(F32), ALU.subtract).then_inc(gs_low, 1)

            def gated_x(s, e):
                dve.wait_ge(wg_ready, EH * (s.n + 1) + e + 1)
                ge = by_chunk_step(flat(g[1 - s.par][:, e, :, :]))
                dve.tensor_tensor(ge, in_time(xT[:, e, :]), ge, ALU.mult).then_inc(g_ready, 1)

            def decayed_mod(s):
                dve.wait_ge(mod_ready, s.n + 1)
                dve.wait_ge(g_ready, EH * (s.n + 1))
                dve.tensor_tensor(decmod[:], chunks_of(mod[s.par][:]),
                                  revpow[:, None, :, None].to_broadcast([P, SEQ, L, NK - 1]), ALU.mult).then_inc(decmod_ready, 1)

            def parts_rest(s):
                dve.wait_ge(decmod_ready, s.n + 1)
                dve.wait_ge(parts_high, 6 * (s.n + 1))
                dve.tensor_tensor(steps_of(modparts[:, :, :, 2, :]), decmod[:], steps_of(modparts[:, :, :, 0, :]).bitcast(F32),
                                  ALU.subtract).then_inc(parts_low, 1)
                for e in range(EH):
                    dve.tensor_tensor(steps_of(gparts[:, e, :, :, 1, :]), chunks_of(g[s.par][:, e, :, :]),
                                      steps_of(gparts[:, e, :, :, 0, :]).bitcast(F32), ALU.subtract).then_inc(parts_low, 1)

            def norm_stats(src, h, st, mv_, ve_, done, before):
                for i in range(2):
                    dve.bn_stats(st[:, 2 * h + i, :], src[i]).then_inc(done, 1)
                dve.wait_ge(done, before + 2)
                dve.memset(waited[:], 0.0)
                for i in range(2):
                    dve.bn_aggr(mv_[:, 2 * h + i, :], st[:, 2 * h + i, :]).then_inc(done, 1)
                dve.wait_ge(done, before + 4)
                dve.tensor_scalar(ve_[:, 2 * h:2 * h + 2], mv_[:, 2 * h:2 * h + 2, 1], EPS, None, ALU.add).then_inc(done, 1)

            def first_norm(s, h):
                m = s.n - 1
                if h == 0:
                    dve.wait_ge(rstd_ready, 2 * m)
                    dve.wait_ge(yb_ready, 2 * m)
                    dve.wait_ge(stored, 16 * m)
                    dve.wait_ge(act_filled, s.a0)
                dve.wait_ge(dve_filled, s.dve("out", h) + 1)
                bank = v_bank(s, "out", h)
                src = [bank[:, i * E:(i + 1) * E] for i in range(2)]
                norm_stats(src, h, stats, mv, ve, stats_done, 10 * m + 5 * h)
                for i in range(2):
                    q = dve.scalar_tensor_tensor(y[:, 2 * h + i, :], src[i], mv[:, 2 * h + i, 0:1], gam0[:],
                                                 ALU.subtract, ALU.mult)
                q.then_inc(dve_taken, 1)

            def first_residual(s, h):
                if h == 0:
                    dve.wait_ge(xbeta_ready, s.n)
                dve.wait_ge(dve_taken, s.dve("out", h) + 1)
                dve.wait_ge(rstd_ready, 2 * (s.n - 1) + 1 + h)
                for p in (2 * h, 2 * h + 1):
                    dve.scalar_tensor_tensor(y[:, p, :], y[:, p, :], rstd[:, p:p + 1], xn[:, p, :],
                                             ALU.mult, ALU.add).then_inc(y_ready, 1)

            def second_norm(s, h):
                m = s.n - 1
                r = rows
                if h == 0:
                    dve.wait_ge(yb_ready, 2 * s.n)
                    dve.wait_ge(rstd2_ready, 2 * m)
                two = slice(2 * h, 2 * h + 2)
                dve.wait_ge(dve_filled, s.dve("w2", h) + 1)
                dve.tensor_tensor(z[:, two, :], v_bank(s, "w2", h)[:].rearrange("t (i c) -> t i c", i=2), r[:, two, 0, :],
                                  ALU.add).then_inc(dve_taken, 1)
                dve.wait_ge(dve_taken, s.dve("w2", h) + 1)
                norm_stats([z[:, 2 * h + i, :] for i in range(2)], h, stats2, mv2, ve2, stats2_done, 14 * m + 7 * h)
                for i in range(2):
                    p = 2 * h + i
                    q = dve.scalar_tensor_tensor(z[:, p, :], z[:, p, :], mv2[:, p, 0:1], r[:, p, 1, :],
                                                 ALU.subtract, ALU.mult)
                    q.then_inc(stats2_done, 1)

            def second_residual(s, h):
                m = s.n - 1
                dve.wait_ge(rstd2_ready, 2 * m + 1 + h)
                for p in (2 * h, 2 * h + 1):
                    dve.wait_ge(stats2_done, 14 * m + 7 * (p // 2) + 6 + p % 2)
                    dve.scalar_tensor_tensor(z[:, p, :], z[:, p, :], rstd2[:, p:p + 1], rows[:, p, 2, :],
                                             ALU.mult, ALU.add).then_inc(out_ready, 1)

            def blended_sums(s, p, i):
                if i == 0:
                    if p == 2:
                        dve.wait_ge(act_filled, s.act("carry", 0) + 1)
                    elif p == 0 and s is not FIRST:
                        dve.wait_ge(act_filled, s.a0)
                dve.wait_ge(dve_filled, s.dve(f"chunk{p}", i) + 1)
                j, n = (0, 2) if i < 2 else (2, 1)
                dve.tensor_tensor(blended[:, p % 2, i % 2, j:j + n, :],
                                  v_bank(s, f"chunk{p}", i)[:, 0:n * E].rearrange("d (j c) -> d j c", j=n),
                                  bw[:, None, :].to_broadcast([P, n, E]), ALU.mult).then_inc(dve_taken, 1)

            def add_carried(s, i):
                if i == 0:
                    dve.wait_ge(lags_added, LAG_ADDS * (s.n + 1))
                dve.wait_ge(dve_filled, s.dve("carryT", i) + 1)
                bank = v_bank(s, "carryT", i)
                sums = temporal[s.par][:].rearrange("c e b (p k) -> c e (b p) k", k=NK)
                half = SEQ // 2 * L
                if i == 0:
                    to, col = sums[:, :, 0:half, 2:NK], 0
                else:
                    to, col = sums[:, :, :, 1], 0
                    dve.tensor_tensor(to, to, bank[:, 0:E].rearrange("c (e r) -> c e r", e=EH), ALU.add)
                    to, col = sums[:, :, half:, 2:NK], E
                dve.tensor_tensor(to, to, bank[:, col:col + E].rearrange("c (e r k) -> c e r k", e=EH, k=2), ALU.add)\
                    .then_inc(dve_taken, 1)

            def one_pass(s):
                def heavy(stage, *k):
                    if s.heavy:
                        stage(s, *k)

                def tail(stage, *k):
                    if s.tail:
                        stage(s, *k)

                def front(stage, *k):
                    if s.front:
                        stage(s, *k)

                heavy(lag_products, 0, 0, 1)
                heavy(decayed_mod)
                heavy(lag_products, 0, 1, 5)
                heavy(parts_rest)
                tail(gated_soma, 0)
                tail(gated_soma, 1)
                heavy(lag_products, 0, 5, 6)
                tail(gs_rest, 0)
                tail(gs_rest, 1)
                heavy(lag_products, 0, 6, 8)
                tail(first_norm, 0)
                tail(first_norm, 1)
                heavy(lag_products, 0, 8, 9)
                tail(first_residual, 0)
                heavy(lag_products, 1, 0, 1)
                tail(first_residual, 1)
                heavy(lag_products, 1, 1, 2)
                front(gate_scan, 0)
                for i in range(0, 2):
                    heavy(blended_sums, 0, i)
                heavy(lag_products, 1, 2, 3)
                for i in range(2, 4):
                    heavy(blended_sums, 0, i)
                heavy(lag_products, 1, 3, 4)
                for i in range(0, 3):
                    heavy(blended_sums, 1, i)
                front(gated_x, 0)
                heavy(blended_sums, 1, 3)
                heavy(lag_products, 1, 4, 7)
                tail(second_norm, 0)
                for i in range(0, 4):
                    heavy(blended_sums, 2, i)
                tail(second_norm, 1)
                front(gate_scan, 1)
                for i in range(0, 3):
                    heavy(blended_sums, 3, i)
                heavy(lag_products, 1, 7, 8)
                heavy(blended_sums, 3, 3)
                heavy(lag_products, 1, 8, 9)
                front(gated_x, 1)
                tail(second_residual, 0)
                heavy(add_carried, 0)
                heavy(add_carried, 1)
                tail(second_residual, 1)

            count = [0]

            def step(instruction):
                count[0] += 1
                instruction.then_inc(dve_const, 1)
                dve.wait_ge(dve_const, count[0])

            a, ac = alpha[:, 0:1], alpha[:, 1:2]
            step(dve.memset(decay[:], 1.0))
            dve.wait_ge(act_const, ACT_ALPHA)
            step(dve.tensor_scalar(decay[:], decay[:], ac, None, ALU.mult))
            step(dve.memset(decay[:].rearrange("c (b t) -> c b t", t=T)[:, :, 0:1], 0.0))
            dve.wait_ge(pe_const, PE_TURNED)
            step(dve.tensor_reduce(smax[:], vbank[2][:, 0:EH * P].rearrange("c (e d) -> c e d", e=EH), AX.X, ALU.max))
            step(dve.tensor_scalar(smax[:], smax[:], -1.0, None, ALU.mult))
            assert count[0] == DVE_MAX, count
            step(dve.tensor_copy(powsq[:, 0:1], a))
            for i in range(1, 6):
                step(dve.tensor_tensor(powsq[:, i:i + 1], powsq[:, i - 1:i], powsq[:, i - 1:i], ALU.mult))
            step(dve.memset(revpow[:, L - 1:L], 1.0))
            for i in range(4):
                m = 1 << i
                step(dve.tensor_scalar(revpow[:, L - 2 * m:L - m], revpow[:, L - m:L], powsq[:, i:i + 1], None, ALU.mult))
            step(dve.tensor_copy(pows[:, 1:2], a))
            for i in range(6):
                m = 1 << i
                step(dve.tensor_scalar(pows[:, m + 1:2 * m + 1], pows[:, 1:m + 1], powsq[:, i:i + 1], None, ALU.mult))
            assert count[0] == DVE_POWERS, count
            dve.wait_ge(weights_loaded, 16 * WEIGHT_LOADS)
            step(dve.tensor_tensor(wg_raw[:, 1, :, :], wg_raw[:, 1, :, :], wg_raw[:, 0, :, :], ALU.add))
            step(dve.tensor_scalar(wg_raw[:, 0, :, :], wg_raw[:, 0, :, :], ac, -1.0, ALU.mult, ALU.mult))
            assert count[0] == DVE_SUMS, count
            dve.wait_ge(act_const, ACT_EXP)
            step(dve.reciprocal(srec[:], ssum[:]))
            for e in range(EH):
                step(dve.tensor_scalar(soma[1][:, e, 0:P], soma[1][:, e, 0:P], srec[:, e:e + 1], None, ALU.mult))
            assert count[0] == DVE_SOFTMAX, count
            dve.wait_ge(act_const, ACT_WEIGHTS)
            for w, exact in ((wn1[:], wn1_raw), (ws[:], ws_raw), (wg[:].rearrange("c s a k e -> c s (a k) e"),
                                                                 wg_raw.rearrange("c a k e -> c (a k) e"))):
                step(dve.tensor_tensor(w[:, 1, :, :], exact, w[:, 0, :, :].bitcast(F32), ALU.subtract))
            assert count[0] == DVE_WEIGHTS, count
            dve.wait_ge(pe_const, PE_BLEND)
            step(dve.tensor_copy(bw, vbank[3][:, 0:E]))

            def decayed(to, lag):
                n = to.shape[1]
                step(dve.tensor_tensor(to, bw[:, None, :].to_broadcast([P, n, E]),
                                       pows[:, lag:lag + n, None].to_broadcast([P, n, E]), ALU.mult))

            decayed(lagw_raw, 1)
            step(dve.tensor_copy(lagw[:, 0, 0, :], bw))
            step(dve.tensor_copy(lagw[:, 0, 1:LAGS, :], lagw_raw))
            assert count[0] == DVE_LAGS, count
            decayed(lagw_far[:], LAGS)
            dve.wait_ge(const_loaded, 16 * CONST_LOADS)
            dve.wait_ge(pool_const, 3)
            step(dve.tensor_copy(lang[:], lang_i[:]))
            step(dve.tensor_copy(idf, ids_l))
            step(dve.tensor_scalar(onehot, idf, lang[:], None, ALU.is_equal))
            assert count[0] == DVE_ALL, count
            one_pass(FILL)
            dve.wait_ge(pool_const, POOL_LAGS)
            one_pass(FIRST)
            one_pass(SECOND)
            with dve.Fori(0, LOOPS) as j:
                for u in range(2):
                    one_pass(loop_pass(j, u))
            one_pass(SECOND_LAST)
            one_pass(LAST)
            one_pass(DRAIN)


def kernel(x, condB_tauraws, cond_256, condB_bn2, cond_1024, itok_B_0_8, L0_cond_tau_ctx, L0_cond_Wg, L0_cond_bg,
           L0_cond_Wn1, L0_cond_bn1, L0_cond_Wsoma, L0_cond_bsoma, L0_cond_Wtemp, L0_cond_btemp, L0_cond_Wout,
           L0_cond_gamma, L0_cond_beta, L1_cond_W1, L1_cond_b1, L1_cond_W2, L1_cond_b2, L1_cond_gamma, L1_cond_beta):
    import numpy as np
    import concourse.bacc as bacc
    from concourse.bass_utils import run_bass_kernel_spmd

    def turned(a):
        return np.ascontiguousarray(np.asarray(a).T)

    rows = np.asarray(x).reshape(B * T, E)
    vectors = np.concatenate([np.asarray(a) for a in (L0_cond_bg, L0_cond_bsoma, L0_cond_btemp, L0_cond_bn1, L0_cond_bn1,
                                                      condB_bn2, np.broadcast_to(L0_cond_tau_ctx, P), condB_tauraws)])
    cols = turned(vectors.reshape(-1, P))
    inputs = [
        ("xT", turned(rows)), ("x", rows), ("cols", cols), ("wn2T", turned(cond_256)),
        ("blend", cond_1024), ("ids", np.asarray(itok_B_0_8).reshape(1, B)), ("wgT", turned(L0_cond_Wg)),
        ("wn1T", turned(L0_cond_Wn1)), ("wsT", turned(L0_cond_Wsoma)), ("wtT", turned(L0_cond_Wtemp)),
        ("woT", turned(L0_cond_Wout)), ("gamma", L0_cond_gamma), ("beta", L0_cond_beta),
        ("w1", L1_cond_W1), ("b1", L1_cond_b1), ("w2", L1_cond_W2),
        ("rows", np.concatenate([np.asarray(a) for a in (L1_cond_b2, L1_cond_gamma, L1_cond_beta)], axis=1)),
    ]
    nc = bacc.Bacc("TRN2", target_bir_lowering=False, num_devices=1)
    arrays, args = {}, []
    for name, a in inputs:
        a = np.ascontiguousarray(a)
        arrays[f"in_{name}"] = a
        args.append(nc.dram_tensor(f"in_{name}", a.shape, mybir.dt.from_np(a.dtype), kind="ExternalInput").ap())
    out = nc.dram_tensor("out_dram", (B * T, E), F32, kind="ExternalOutput").ap()
    build(nc, *args, out)
    r = run_bass_kernel_spmd(nc, [arrays], core_ids=[0])
    return r.results[0]["out_dram"].reshape(B, T, E)
```
